# Optimizing a Trainium2 kernel written in Bass

```python
import numpy as np
import jax
import jax.numpy as jnp

def _softmax(x, axis=-1):
    return jax.nn.softmax(x, axis=axis)

def _gelu(x):
    return jax.nn.gelu(x, approximate=True)

def _silu(x):
    return jax.nn.silu(x)

def _sigmoid(x):
    return jax.nn.sigmoid(x)

def _layernorm(x, axis=-1, eps=1e-05):
    m = jnp.mean(x, axis=axis, keepdims=True)
    v = jnp.var(x, axis=axis, keepdims=True)
    return (x - m) / jnp.sqrt(v + eps)

def _scatter_add(tgt, idx, src, axis=0):
    return tgt.at[idx].add(src)

def _segment_sum(src, seg, n):
    return jax.ops.segment_sum(src, seg, n)
kernel_name = 'mk_seq_postln_d1_jaxref_r4_fd86f1'

def setup_inputs(seed: int=0):
    np.random.seed(seed)
    _w = jnp.asarray

    def _L0_attn_setup():
        import math
        import jax, jax.numpy as jnp
        import numpy as np
        N_HEADS = 16
        D_EMBED = 256
        key = jax.random.key(seed)
        ks = jax.random.split(key, 5)
        b, l, d = (2, 512, D_EMBED)
        return {'x': jax.random.normal(ks[0], (b, l, d), dtype=jnp.float32), 'w_in': jax.random.normal(ks[1], (3 * d, d), dtype=jnp.float32) * 0.02, 'b_in': jax.random.normal(ks[2], (3 * d,), dtype=jnp.float32) * 0.02, 'w_out': jax.random.normal(ks[3], (d, d), dtype=jnp.float32) * 0.02, 'b_out': jax.random.normal(ks[4], (d,), dtype=jnp.float32) * 0.02}
    _L0_attn_in = _L0_attn_setup()

    def _L0_ffn_setup():
        import jax, jax.numpy as jnp
        import numpy as np
        N_HEAD = 16
        N_ACTIVE = 4
        D_MODEL = 256
        D_ATTN = 64
        B = 4
        S = 512
        key = jax.random.key(seed)
        ks = jax.random.split(key, 6)
        sc = 1.0 / np.sqrt(D_MODEL).astype(np.float32)
        return {'x': jax.random.normal(ks[0], (B, S, D_MODEL), jnp.float32), 'Wq': jax.random.normal(ks[1], (D_MODEL, N_HEAD * D_ATTN), jnp.float32) * sc, 'bq': jnp.zeros((N_HEAD * D_ATTN,), jnp.float32), 'Wk': jax.random.normal(ks[2], (D_MODEL, N_HEAD * D_ATTN), jnp.float32) * sc, 'bk': jnp.zeros((N_HEAD * D_ATTN,), jnp.float32), 'Wv': jax.random.normal(ks[3], (D_MODEL, N_HEAD * D_ATTN), jnp.float32) * sc, 'bv': jnp.zeros((N_HEAD * D_ATTN,), jnp.float32), 'Wr': jax.random.normal(ks[4], (D_MODEL, N_HEAD), jnp.float32) * sc, 'br': jnp.zeros((N_HEAD,), jnp.float32), 'Wo': jax.random.normal(ks[5], (N_ACTIVE * D_ATTN, D_MODEL), jnp.float32) * (1.0 / np.sqrt(N_ACTIVE * D_ATTN).astype(np.float32)), 'bo': jnp.zeros((D_MODEL,), jnp.float32)}
    _L0_ffn_in = _L0_ffn_setup()
    _d = {'L0_attn_x': _L0_attn_in['x'], 'L0_attn_w_in': _L0_attn_in['w_in'], 'L0_attn_b_in': _L0_attn_in['b_in'], 'L0_attn_w_out': _L0_attn_in['w_out'], 'L0_attn_b_out': _L0_attn_in['b_out'], 'L0_ffn_Wq': _L0_ffn_in['Wq'], 'L0_ffn_bq': _L0_ffn_in['bq'], 'L0_ffn_Wk': _L0_ffn_in['Wk'], 'L0_ffn_bk': _L0_ffn_in['bk'], 'L0_ffn_Wv': _L0_ffn_in['Wv'], 'L0_ffn_bv': _L0_ffn_in['bv'], 'L0_ffn_Wr': _L0_ffn_in['Wr'], 'L0_ffn_br': _L0_ffn_in['br'], 'L0_ffn_Wo': _L0_ffn_in['Wo'], 'L0_ffn_bo': _L0_ffn_in['bo']}
    _x0 = _d['L0_attn_x']
    _d['L0_attn_x'] = jax.random.normal(jax.random.fold_in(jax.random.key(seed), 1), (4, 2048, 256), dtype=_x0.dtype)
    del _x0
    return _d

def reference(L0_attn_x, L0_attn_w_in, L0_attn_b_in, L0_attn_w_out, L0_attn_b_out, L0_ffn_Wq, L0_ffn_bq, L0_ffn_Wk, L0_ffn_bk, L0_ffn_Wv, L0_ffn_bv, L0_ffn_Wr, L0_ffn_br, L0_ffn_Wo, L0_ffn_bo):

    def _L0_attn_ref(x, w_in, b_in, w_out, b_out):
        import math
        import jax, jax.numpy as jnp
        import numpy as np
        N_HEADS = 16
        D_EMBED = 256
        b, l, d = x.shape
        h = N_HEADS
        scale = 1.0 / math.sqrt(d // h)
        x_proj = (x @ w_in.T + b_in).reshape(b, l, h, -1)
        q, k, v = jnp.split(x_proj, 3, axis=-1)
        att = jnp.einsum('blhd,bmhd->blmh', q, k) * scale
        att = jax.nn.softmax(att, axis=2)
        opt = jnp.einsum('blmh,blhd->blhd', att, v).reshape(b, l, d)
        return opt @ w_out.T + b_out

    def _L0_ffn_ref(x, Wq, bq, Wk, bk, Wv, bv, Wr, br, Wo, bo):
        import jax, jax.numpy as jnp
        import numpy as np
        N_HEAD = 16
        N_ACTIVE = 4
        D_MODEL = 256
        D_ATTN = 64
        B = 4
        S = 512
        b, s, _ = x.shape
        dist = jax.nn.softmax(jnp.mean(x @ Wr + br, axis=1), axis=-1)
        _, idx = jax.lax.top_k(dist, N_ACTIVE)
        idx = jnp.sort(idx, axis=-1)

        def proj(W, bias):
            return (x @ W + bias).reshape(b, s, N_HEAD, D_ATTN).transpose(0, 2, 1, 3)
        Q = proj(Wq, bq)
        K = proj(Wk, bk)
        V = proj(Wv, bv)
        gather = lambda t: jnp.take_along_axis(t, idx[:, :, None, None], axis=1)
        Qs, Ks, Vs = (gather(Q), gather(K), gather(V))
        scale = 1.0 / jnp.sqrt(jnp.asarray(D_ATTN, x.dtype))
        score = jax.nn.softmax(jnp.einsum('bhqd,bhkd->bhqk', Qs, Ks) * scale, axis=-1)
        O = jnp.einsum('bhqk,bhkd->bhqd', score, Vs)
        O = O.transpose(0, 2, 1, 3).reshape(b, s, N_ACTIVE * D_ATTN)
        return O @ Wo + bo
    x = L0_attn_x
    x = _layernorm(x + _L0_attn_ref(x, L0_attn_w_in, L0_attn_b_in, L0_attn_w_out, L0_attn_b_out), axis=-1)
    x = _layernorm(x + _L0_ffn_ref(x, L0_ffn_Wq, L0_ffn_bq, L0_ffn_Wk, L0_ffn_bk, L0_ffn_Wv, L0_ffn_bv, L0_ffn_Wr, L0_ffn_br, L0_ffn_Wo, L0_ffn_bo), axis=-1)
    return x

_drawn_inputs = setup_inputs


def setup_inputs(seed=0):
    import zlib

    import numpy as np

    out = dict(_drawn_inputs(seed))
    spreads = {'L0_ffn_bq': (0.0, 0.8),
     'L0_ffn_bk': (0.0, 0.8),
     'L0_ffn_bv': (0.0, 0.1),
     'L0_ffn_br': (0.0, 0.1),
     'L0_ffn_bo': (0.0, 0.1)}
    factors = {'L0_attn_b_in': 5.613}
    for name, (base, spread) in spreads.items():
        noise = np.random.default_rng([zlib.crc32(name.encode()), seed]).standard_normal(out[name].shape)
        drawn = base * np.exp(spread * noise) if base else spread * noise
        out[name] = jnp.asarray(drawn.astype(out[name].dtype))
    for name, factor in factors.items():
        out[name] = (out[name] * factor).astype(out[name].dtype)
    return out
```

```python
import concourse.bass as bass
from concourse import mybir
from contextlib import ExitStack

F32 = mybir.dt.float32
BF16 = mybir.dt.bfloat16
U32 = mybir.dt.uint32
I32 = mybir.dt.int32
ALU = mybir.AluOpType
ACT = mybir.ActivationFunctionType
AX = mybir.AxisListType
ds = bass.ds

P = 128
B, L, D = 4, 2048, 256
NT = L // P
KC = D // P
CH = 512
NCH = L // CH
TPC = CH // P
AH, AD = 16, D // 16
GH = P // AD
FH, FD = 4, 64
NR = 16
LV = 3
Q_LEVEL = (0, 0, 0, 1, 1, 2)
K_LEVEL = (0, 1, 2, 0, 1, 0)
SK = len(Q_LEVEL) * AD
TILE = 1024
HALF = L // TILE
EPS = 1e-5
SLOTS = 3
A_SLOTS = 4
UNITS = 4
CREDIT = A_SLOTS

BOTH = ("F0", "F1", "A", "A", "T0", "A", "A", "T1", "PV0", "A", "A", "A", "PV1", "A")
ONLY_A = ("A",) * 8
ONLY_F = ("F0", "F1", "T0", "T1", "PV0", "PV1")


def ring_items(unit):
    return [x for x in unit if not x.startswith("PV")]


def build(nc, x, w_in, b_in, w_out, b_out, wq, bq, wk, bk, wv, bv, wr, br, wo, bo, out):
    ctx = ExitStack()
    with ctx:
        sb = lambda name, shape, dt=F32: ctx.enter_context(nc.sbuf_tensor(name, shape, dt))
        sem = lambda name: ctx.enter_context(nc.semaphore(name))
        ctx.enter_context(nc.allow_non_contiguous_dma(reason="bias columns"))

        x1_dram = nc.dram_tensor("x1_rows", [NT, P, D], F32).ap()
        ident = sb("ident", [P, P])
        w_inT = sb("w_inT", [P, KC, 3 * D])
        w_outT = sb("w_outT", [P, KC, D])
        wo_sb = sb("wo_sb", [P, KC, D])
        wr_sb = sb("wr_sb", [P, KC, NR])
        b_in_rows = sb("b_in_rows", [P, 3 * D])
        b_out_rows = sb("b_out_rows", [P, D])
        bo_rows = sb("bo_rows", [P, D])
        br_row = sb("br_row", [1, NR])
        qk_bias = sb("qk_bias", [P, 4])
        wv_sel = sb("wv_sel", [P, KC, FH * FD])
        bv_sel = sb("bv_sel", [P, FH * FD])
        wqk_sel = sb("wqk_sel", [P, KC, 2, 2 * FD])
        bqk_sel = sb("bqk_sel", [P, 2])
        one = sb("one", [1, 1])

        split = sb("split", [P, 2, 2, LV, L], BF16)
        stack = sb("stack", [P, 2, 2, L], BF16)
        fq = sb("fq", [P, 2, 3, L], BF16)
        fk = sb("fk", [P, 2, 2, L], BF16)
        vals = sb("vals", [P, NT, FH, FD + 1])
        x1T = sb("x1T", [P, KC, L])
        fo = sb("fo", [P, NT, FH * FD])
        shared = sb("shared", [P, 2 * L])
        probs = shared[:, 0:L]
        probsT = shared[:, L:2 * L].rearrange("p (f k) -> p f k", f=HALF)
        y = shared[:, :].rearrange("p (t d) -> p t d", t=NT)
        qk32 = shared[:, 0:L].rearrange("p (s n) -> p s n", s=4)
        rest32 = shared[:, L:2 * L].rearrange("p (s n) -> p s n", s=4)
        w_rows = shared[:, 0:6 * D].rearrange("p (t d) -> p t d", t=6)
        w_out_rows = shared[:, 6 * D:8 * D].rearrange("p (t d) -> p t d", t=KC)
        stats32 = shared[:, 0:6 * NT * AH].rearrange("p (s n) -> p s n", s=6)
        buf_a = sb("buf_a", [P, TPC * D])
        buf_b = sb("buf_b", [P, TPC * D])
        buf_c = sb("buf_c", [P, TPC * D])
        rows_in = buf_a[:, :].rearrange("p (t d) -> p t d", t=TPC)
        chunkT = buf_b[:, :].rearrange("p (c n) -> p c n", c=KC)
        rows_mid = buf_c[:, :].rearrange("p (t d) -> p t d", t=TPC)
        f32s = buf_a[:, :].rearrange("p (s n) -> p s n", s=2)
        frest = buf_b[:, :].rearrange("p (s n) -> p s n", s=2)
        fmid = buf_c[:, 0:CH // 2].bitcast(BF16)

        nmax = sb("nmax", [P, HALF, NT, AH])
        esum = sb("esum", [P, HALF, NT, AH])
        att = sb("att", [P, NT, AH])
        fmin = sb("fmin", [P, HALF])
        fnmax = sb("fnmax", [P, 1])
        frec = sb("frec", [P, 1])
        mv = sb("mv", [P, NT, 2])
        st = sb("st", [P, TPC, 6])
        mv_chunk = sb("mv_chunk", [P, TPC, 2])
        var = sb("var", [P, NT])
        rstd = sb("rstd", [P, NT])
        newt = sb("newt", [P, NT])
        xsum = sb("xsum", [P, KC])
        route = sb("route", [1, 4 * NR])
        top_i = sb("top_i", [1, 8], U32)
        head_i = sb("head_i", [1, 8], I32)

        ps = ctx.enter_context(nc.psum_tensor("ps", [P, 8, CH], F32))
        O_BANK, FP_BANK = 6, 7
        bank = lambda n: ps[:, n, :]
        bank_rows = lambda n: ps[:, n, :].rearrange("p (t d) -> p t d", d=D)

        const_in = sem("const_in")
        const_made = sem("const_made")
        wT_ready = sem("wT_ready")
        wT_read = sem("wT_read")
        x_in = sem("x_in")
        x_tr = sem("x_tr")
        xT_ready = sem("xT_ready")
        qk_ready = sem("qk_ready")
        q32_ready = sem("q32_ready")
        k32_ready = sem("k32_ready")
        q_split = sem("q_split")
        k_split = sem("k_split")
        stack_in = [sem("stack_in_even"), sem("stack_in_odd")]
        filled = sem("filled")
        min_ready = sem("min_ready")
        fmin_ready = sem("fmin_ready")
        tile_read = sem("tile_read")
        pv_done = sem("pv_done")
        o_rec = sem("o_rec")
        o_read = sem("o_read")
        comb = sem("comb")
        comb_e = sem("comb_e")
        v_ready = sem("v_ready")
        v_read = sem("v_read")
        o1_ready = sem("o1_ready")
        o1_tr = sem("o1_tr")
        o1T_ready = sem("o1T_ready")
        res_in = sem("res_in")
        res_ready = sem("res_ready")
        yp_ready = sem("yp_ready")
        y_ready = sem("y_ready")
        bn_ready = sem("bn_ready")
        ln = sem("ln")
        ln_sq = sem("ln_sq")
        n_ready = sem("n_ready")
        n_out = sem("n_out")
        x1_tr = sem("x1_tr")
        x1T_ready = sem("x1T_ready")
        rt = sem("rt")
        rt_mm = sem("rt_mm")
        rt_e = sem("rt_e")
        wv_in = sem("wv_in")
        x1c_ready = sem("x1c_ready")
        fv_ready = sem("fv_ready")
        fv_read = sem("fv_read")
        fpw_in = sem("fpw_in")
        fp_ready = sem("fp_ready")
        fp_read = sem("fp_read")
        fsp = sem("fsp")
        fo_stage = sem("fo_stage")

        A_TILES = AH * NT * HALF
        F_TILES = FH * NT * 4
        A_MINS, F_MINS = AH * NT * HALF, FH * NT
        N_BODY = 2 * UNITS
        Q_STEPS = K_STEPS = 4
        LN_STEPS, BN_STEPS = 6, 3
        COMB_STEPS = 6
        ROUTE_STEPS = 11
        N_CONST = 8
        HEAD_DMAS = 12
        SEL_DMAS = 8
        PROJ = (FH + 1) * NCH

        def filled_before(b, mode):
            return b * (A_TILES + F_TILES) + (0 if mode == "A" else A_TILES)

        def read_before(b, mode):
            return filled_before(b, mode) + CREDIT

        def mins_before(b, mode):
            return b * (A_MINS + F_MINS) + (0 if mode == "A" else A_MINS)

        UNIT = {"A": ONLY_A, "F": ONLY_F}
        RING = {"A": A_SLOTS, "F": SLOTS}

        def per_body(mode):
            return len(ring_items(UNIT[mode])) * N_BODY

        def reuse(i, slots, body):
            return i - slots if i >= slots else max(j for j in range(body) if j % slots == i % slots) - body

        def tile_ap(slot):
            return ps[:, 2 * slot:2 * slot + 2, :].rearrange("p a n -> p (a n)")

        def flat(ap):
            return ap.rearrange("p a n -> p (a n)")

        block = ctx.enter_context(nc.Block())

        @block.sync
        def _(sp):
            row = lambda v: v.rearrange("(a n) -> a n", a=1)
            sp.dma_start(w_rows, w_in.rearrange("(t p) d -> p t d", p=P)).then_inc(const_in, 16)
            sp.dma_start(w_out_rows, w_out.rearrange("(t p) d -> p t d", p=P)).then_inc(const_in, 16)
            sp.dma_start(wo_sb[:, :, :], wo.rearrange("(c p) n -> p c n", p=P)).then_inc(const_in, 16)
            sp.dma_start(wr_sb[:, :, :], wr.rearrange("(c p) n -> p c n", p=P)).then_inc(const_in, 16)
            sp.dma_start(b_in_rows[:, :], b_in.partition_broadcast(P)).then_inc(const_in, 16)
            sp.dma_start(b_out_rows[:, :], b_out.partition_broadcast(P)).then_inc(const_in, 16)
            sp.dma_start(bo_rows[:, :], bo.partition_broadcast(P)).then_inc(const_in, 16)
            sp.dma_start(br_row[:, :], row(br)).then_inc(const_in, 16)

            x_rows = x.rearrange("b (t p) d -> (b t) p d", p=P)
            out_tiles = out.rearrange("b (t p) d -> (b t) p d", p=P)

            def load_x(b, phase):
                with sp.Fori(0, NCH) as c:
                    sp.wait_ge(y_ready, b * 2 * NCH + (c if phase else 0))
                    sp.wait_ge(x_tr, (b * 2 * NCH + phase * NCH + c) * TPC)
                    sp.dma_start(rows_in, x_rows[ds((b * NCH + c) * TPC, TPC), :, :].rearrange("t p d -> p t d")
                                 ).then_inc(x_in, 16)

            with sp.Fori(0, B) as b:
                load_x(b, 0)
                head_tiles = per_body("A") // 2
                with sp.Fori(0, 2) as hh:
                    sp.wait_ge(q_split, (b + 1) * NCH * Q_STEPS)
                    sp.wait_ge(k_split, (b + 1) * NCH * K_STEPS)
                    for r in range(GH):
                        sp.wait_ge(filled, filled_before(b, "A") +
                                   (hh * (GH - 1) * head_tiles if r == 0 else (hh * GH + r - 1) * head_tiles))
                        for side, levels in ((0, Q_LEVEL), (1, K_LEVEL)):
                            for g, lv in enumerate(levels):
                                sp.dma_start(stack[g * AD:(g + 1) * AD, r % 2, side, :],
                                             flat(split[r * AD:(r + 1) * AD, side, ds(hh, 1), lv, :])
                                             ).then_inc(stack_in[r % 2], 16)
                load_x(b, 1)
                with sp.Fori(0, NCH) as c:
                    k = b * 2 * NCH + c
                    sp.wait_ge(n_out, k * 16)
                    sp.wait_ge(n_ready, (k + 1) * TPC)
                    sp.dma_start(x1_dram[ds((c + 1) * TPC - TPC, TPC), :, :].rearrange("t p d -> p t d"),
                                 rows_mid).then_inc(n_out, 16)
                with sp.Fori(0, FH) as h:
                    sp.wait_ge(rt, (b + 1) * ROUTE_STEPS)
                    i = sp.value_load(head_i[0:1, ds(h % FH, 1)], min_val=0, max_val=NR - 1)
                    sp.dma_start(wv_sel[:, :, ds(h * FD, FD)],
                                 wv[:, ds(i * FD, FD)].rearrange("(c p) n -> p c n", p=P)).then_inc(wv_in, 16)
                    sp.dma_start(bv_sel[:, ds(h * FD, FD)],
                                 bv[ds(i * FD, FD)].partition_broadcast(P)).then_inc(wv_in, 16)

                with sp.Fori(0, FH + 1) as hh:
                    done = (b * PROJ + hh * NCH) * 2
                    sp.wait_ge(fp_ready, done)
                    sp.wait_ge(fp_read, done)
                    i = sp.value_load(head_i[0:1, ds(hh % FH, 1)], min_val=0, max_val=NR - 1)
                    for s, (w, bias) in enumerate(((wq, bq), (wk, bk))):
                        for twice in range(2):
                            sp.dma_start(wqk_sel[:, :, s, twice * FD:(twice + 1) * FD],
                                         w[:, ds(i * FD, FD)].rearrange("(c p) n -> p c n", p=P)).then_inc(fpw_in, 16)
                            sp.dma_start(bqk_sel[twice * FD:(twice + 1) * FD, s:s + 1],
                                         bias[ds(i * FD, FD)].rearrange("(p a) -> p a", a=1)).then_inc(fpw_in, 16)

                with sp.Fori(0, NCH) as c:
                    sp.wait_ge(fsp, (b + 1) * PROJ)
                    sp.wait_ge(y_ready, (b * 2 + 1) * NCH + c)
                    sp.dma_start(rows_in, x1_dram[ds(c * TPC, TPC), :, :].rearrange("t p d -> p t d")
                                 ).then_inc(res_in, 16)
                with sp.Fori(0, NCH) as c:
                    k = (b * 2 + 1) * NCH + c
                    sp.wait_ge(n_out, k * 16)
                    sp.wait_ge(n_ready, (k + 1) * TPC)
                    sp.dma_start(out_tiles[ds((b * NCH + c) * TPC, TPC), :, :].rearrange("t p d -> p t d"),
                                 rows_mid).then_inc(n_out, 16)
            sp.wait_ge(n_out, B * 2 * NCH * 16)

        @block.gpsimd
        def _(pool):
            pool.memset(ident[:, :], 0.0).then_inc(const_made, 1)
            pool.memset(one[:, :], 1.0).then_inc(const_made, 1)
            pool.memset(vals[:, :, :, FD:FD + 1], 1.0).then_inc(const_made, 1)
            pool.wait_ge(const_made, 3)
            pool.affine_select(out=ident[:, :], in_=ident[:, :], compare_op=ALU.not_equal, fill=1.0, base=0,
                               pattern=[[-1, P]], channel_multiplier=1).then_inc(const_made, 1)
            with pool.Fori(0, B) as b:
                pool.wait_ge(const_in, 16 * N_CONST)
                with pool.Fori(0, NCH) as c:
                    pool.wait_ge(filled, filled_before(b, "A"))
                    k = b * NCH + c
                    level = lambda lv: split[:, 1, :, lv, ds(c * CH, CH)]
                    keys, rest = qk32[:, 2:4, :], rest32[:, 2:4, :]
                    pool.wait_ge(k32_ready, k * 2 + 2)
                    pool.tensor_copy(level(0), keys).then_inc(k_split, 1)
                    pool.drain()
                    pool.tensor_tensor(rest, keys, level(0), ALU.subtract).then_inc(k_split, 1)
                    pool.drain()
                    pool.tensor_copy(level(1), rest).then_inc(k_split, 1)
                    pool.drain()
                    pool.tensor_tensor(level(2), rest, level(1), ALU.subtract).then_inc(k_split, 1)
                with pool.Fori(0, NCH) as c:
                    pool.wait_ge(x_tr, (b * 2 * NCH + NCH + c + 1) * TPC)
                    pool.tensor_tensor(rows_in, rows_in, b_out_rows[:, :].unsqueeze(1).to_broadcast([P, TPC, D]),
                                       ALU.add).then_inc(res_ready, 1)
                with pool.Fori(0, NCH) as c:
                    pool.wait_ge(x1T_ready, (b + 1) * NCH)
                    pool.wait_ge(yp_ready, b * 2 * NCH + NCH)
                    pool.wait_ge(fv_ready, b * NCH + c)
                    pool.tensor_copy(chunkT, x1T[:, :, ds(c * CH, CH)]).then_inc(x1c_ready, 1)

                def split_head(hh, par, spare):
                    with pool.Fori(0, NCH) as c:
                        k = b * PROJ + hh * NCH + c
                        H = P // 2
                        low, high, every = (0, H), (H, P), (0, P)
                        q_to = lambda i, r: flat(fq[r[0]:r[1], ds(par, 1), i, ds(c * CH, CH)])
                        k_to = lambda i, r: flat(fk[r[0]:r[1], ds(par, 1), i, ds(c * CH, CH)])
                        q32, k32 = (lambda r: f32s[r[0]:r[1], 0, :]), (lambda r: f32s[r[0]:r[1], 1, :])
                        qr, kr = (lambda r: frest[r[0]:r[1], 0, :]), (lambda r: frest[r[0]:r[1], 1, :])
                        pool.wait_ge(fv_ready, (b + 1) * NCH)
                        pool.wait_ge(n_out, (b * 2 + 1) * NCH * 16)
                        pool.wait_ge(fp_read, k * 2 + 2)
                        pool.wait_ge(filled, filled_before(b, "F") + (hh - 1) * 2 * per_body("F") if spare else
                                     filled_before(b, "F"))
                        pool.tensor_copy(q_to(0, every), q32(every))
                        pool.drain()
                        pool.tensor_tensor(qr(every), q32(every), q_to(0, every), ALU.subtract)
                        pool.drain()
                        pool.tensor_copy(q_to(1, every), qr(every))
                        pool.drain()
                        pool.tensor_copy(q_to(2, low), q32(low))
                        pool.tensor_copy(k_to(0, low), k32(low))
                        pool.drain()
                        pool.tensor_tensor(kr(low), k32(low), k_to(0, low), ALU.subtract)
                        pool.drain()
                        pool.tensor_copy(fmid[0:H, :], kr(low))
                        pool.drain()
                        pool.tensor_tensor(k_to(1, low), kr(low), fmid[0:H, :], ALU.subtract)
                        pool.drain()
                        pool.tensor_copy(k_to(1, high), k32(high))
                        pool.tensor_tensor(q_to(2, high), qr(high), q_to(1, high), ALU.subtract)
                        pool.drain()
                        pool.tensor_tensor(kr(high), k32(high), k_to(1, high), ALU.subtract)
                        pool.drain()
                        pool.tensor_copy(k_to(0, high), kr(high)).then_inc(fsp, 1)
                        pool.drain()
                split_head(0, 0, False)
                with pool.Fori(0, FH) as h:
                    split_head(h + 1, (h + 1) % 2, True)
                with pool.Fori(0, NCH) as c:
                    pool.wait_ge(o_read, (b + 1) * FH * NT)
                    k = (b * 2 + 1) * NCH + c
                    pool.wait_ge(o1_tr, k)
                    pool.tensor_copy(rows_mid, fo[:, ds(c * TPC, TPC), :]).then_inc(fo_stage, 1)
                    pool.wait_ge(res_in, (b * NCH + c + 1) * 16)
                    pool.tensor_tensor(rows_in, rows_in, bo_rows[:, :].unsqueeze(1).to_broadcast([P, TPC, D]),
                                       ALU.add).then_inc(res_ready, 1)

        @block.tensor
        def _(pe):
            pe.wait_ge(const_made, 4)
            pe.wait_ge(const_in, 16 * N_CONST)
            for cc in range(KC):
                for t in range(6):
                    col = cc * 2 * CH + t * P
                    pe.transpose(ps[:, col // CH, col % CH:col % CH + P],
                                 w_rows[:, t, cc * P:(cc + 1) * P], ident[:, :])
                for t in range(KC):
                    last = pe.transpose(ps[:, 4 + cc, t * P:(t + 1) * P],
                                        w_out_rows[:, t, cc * P:(cc + 1) * P], ident[:, :])
            last.then_inc(wT_ready, 1)
            pe.wait_ge(wT_read, 1)
            for s in range(4):
                last = pe.matmul(ps[:, 6, s:s + 1], buf_c[0:1, s * P:(s + 1) * P], one[:, :],
                                 start=True, stop=True)
            last.then_inc(wT_ready, 1)
            pe.wait_ge(wT_read, 2)

            with pe.Fori(0, B) as b:
                def transpose_x(k):
                    pe.wait_ge(x_in, (k + 1) * 16)
                    for cc in range(KC):
                        for t in range(TPC):
                            last = pe.transpose(ps[:, cc, t * P:(t + 1) * P],
                                                rows_in[:, t, cc * P:(cc + 1) * P], ident[:, :])
                    last.then_inc(x_tr, TPC)
                    pe.wait_ge(xT_ready, k + 1)

                def project_rows(done, w, bank0):
                    for t in range(TPC):
                        for cc in range(KC):
                            last = pe.matmul(ps[:, bank0 + t // 2, (t % 2) * D:(t % 2 + 1) * D],
                                             chunkT[:, cc, t * P:(t + 1) * P], w[:, cc, :],
                                             start=(cc == 0), stop=(cc == KC - 1))
                    last.then_inc(done, 1)

                def transpose_rows(done, bank0):
                    for cc in range(KC):
                        for t in range(TPC):
                            last = pe.transpose(ps[:, bank0 + cc, t * P:(t + 1) * P],
                                                rows_mid[:, t, cc * P:(cc + 1) * P], ident[:, :])
                    last.then_inc(done, 1)

                with pe.Fori(0, NCH) as c:
                    pe.wait_ge(n_ready, (b * 2 * NCH) * TPC)
                    k = b * NCH + c
                    transpose_x(b * 2 * NCH + c)
                    pe.wait_ge(q32_ready, k)
                    pe.wait_ge(k32_ready, k * 2)
                    for s in range(4):
                        for cc in range(KC):
                            last = pe.matmul(bank(2 + s), w_inT[:, cc, s * P:(s + 1) * P], chunkT[:, cc, :],
                                             start=(cc == 0), stop=(cc == KC - 1))
                        last.then_inc(qk_ready, 1)

                def scores(mode, h, qp):
                    it = h * 2 + qp
                    body, slots = per_body(mode), RING[mode]
                    start = read_before(b, mode) + it * body
                    if mode == "A":
                        pe.wait_ge(q32_ready, (b + 1) * NCH)
                        pe.wait_ge(k32_ready, (b + 1) * NCH * 2)
                    else:
                        pe.wait_ge(fv_read, (b + 1) * NCH)
                        pe.wait_ge(fsp, (b * PROJ + (h + 1) * NCH))
                    i = 0
                    for par in range(2):
                        if mode == "A":
                            pe.wait_ge(stack_in[par], (b * (AH // 2) + it + 1) * HEAD_DMAS * 16)
                        for jj in range(UNITS):
                            u = par * UNITS + jj
                            at, ai = {}, 0
                            for item in UNIT[mode]:
                                if item[:2] == "PV":
                                    f = int(item[2])
                                    pe.wait_ge(tile_read, start + at[f"T{f}"] + 1)
                                    if f == 0:
                                        pe.wait_ge(o_read, b * FH * NT + it * N_BODY + u)
                                    for kt in range(NT // 2):
                                        last = pe.matmul(
                                            ps[:, O_BANK, 0:FD + 1], probsT[:, f, kt * P:(kt + 1) * P],
                                            flat(vals[:, f * (NT // 2) + kt, ds(h, 1), :]),
                                            start=(f == 0 and kt == 0), stop=(f == 1 and kt == NT // 2 - 1))
                                    last.then_inc(pv_done, 1)
                                    continue
                                slot = i % slots
                                pe.wait_ge(tile_read, start + reuse(i, slots, body) + 1)
                                at[item] = i
                                if item == "T0":
                                    pe.wait_ge(tile_read, start + at["F1"] + 1)
                                for j in range(2):
                                    n = 2 * slot + j
                                    if item == "A":
                                        t, col = TPC * jj + ai // HALF, (ai % HALF) * TILE + j * CH
                                        last = pe.matmul(bank(n), stack[0:SK, par, 0, t * P:(t + 1) * P],
                                                         stack[0:SK, par, 1, col:col + CH], start=True, stop=True)
                                    elif item[0] == "F":
                                        col = int(item[1]) * TILE + j * CH
                                        for s in range(3):
                                            last = pe.matmul(bank(n), flat(fq[:, ds(h % 2, 1), s, ds(qp * TILE + u * P, P)]),
                                                             flat(fk[:, ds(h % 2, 1), s // 2, col:col + CH]),
                                                             start=(s == 0), stop=(s == 2))
                                    else:
                                        col = int(item[1]) * TILE + j * CH
                                        for kt in range(TPC):
                                            last = pe.transpose(ps[:, n, kt * P:(kt + 1) * P],
                                                                probs[:, col + kt * P:col + (kt + 1) * P], ident[:, :])
                                last.then_inc(filled, 1)
                                ai += item == "A"
                                i += 1

                with pe.Fori(0, FH) as h:
                    with pe.Fori(0, 2) as qp:
                        scores("A", h, qp)

                with pe.Fori(0, NCH) as c:
                    pe.wait_ge(tile_read, read_before(b, "A") + A_TILES)
                    k = b * 2 * NCH + c
                    transpose_x(k + NCH)
                    pe.wait_ge(v_read, b * NCH + c)
                    project_rows(v_ready, w_inT[:, :, 2 * D:3 * D], 2)
                    pe.wait_ge(o1_ready, b * NCH + c + 1)
                    transpose_rows(o1_tr, 4)
                    pe.wait_ge(o1T_ready, k + 1)
                    pe.wait_ge(y_ready, k)
                    project_rows(yp_ready, w_outT, 6)
                with pe.Fori(0, NCH) as c:
                    pe.wait_ge(n_ready, (b * 2 * NCH + c + 1) * TPC)
                    pe.wait_ge(x1T_ready, b * NCH + c)
                    transpose_rows(x1_tr, 0)
                pe.wait_ge(rt, b * ROUTE_STEPS + 1)
                for cc in range(KC):
                    last = pe.matmul(ps[0:1, 2, 0:NR], xsum[:, cc:cc + 1], wr_sb[:, cc, :],
                                     start=(cc == 0), stop=(cc == KC - 1))
                last.then_inc(rt_mm, 1)
                with pe.Fori(0, NCH) as c:
                    pe.wait_ge(wv_in, (b + 1) * 2 * FH * 16)
                    pe.wait_ge(x1c_ready, b * NCH + c + 1)
                    pe.wait_ge(fv_read, b * NCH + c)
                    project_rows(fv_ready, wv_sel, 4)

                def project_head(hh):
                    with pe.Fori(0, NCH) as c:
                        pe.wait_ge(fpw_in, (b * (FH + 1) + hh + 1) * SEL_DMAS * 16)
                        k = b * PROJ + hh * NCH + c
                        for s in range(2):
                            pe.wait_ge(fp_read, k * 2 + s)
                            for cc in range(KC):
                                last = pe.matmul(bank(FP_BANK), wqk_sel[:, cc, s, :], x1T[:, cc, ds(c * CH, CH)],
                                                 start=(cc == 0), stop=(cc == KC - 1))
                            last.then_inc(fp_ready, 1)
                project_head(0)
                with pe.Fori(0, FH) as h:
                    project_head(h + 1)
                    with pe.Fori(0, 2) as qp:
                        scores("F", h, qp)

                with pe.Fori(0, NCH) as c:
                    pe.wait_ge(tile_read, read_before(b, "F") + F_TILES)
                    k = (b * 2 + 1) * NCH + c
                    pe.wait_ge(fo_stage, b * NCH + c + 1)
                    transpose_rows(o1_tr, 4)
                    pe.wait_ge(o1T_ready, k + 1)
                    pe.wait_ge(y_ready, k)
                    project_rows(yp_ready, wo_sb, 6)

        @block.scalar
        def _(act):
            act.wait_ge(const_made, 4)
            act.activation(frec[0:1, :], one[:, :], ACT.Copy).then_inc(tile_read, CREDIT)
            with act.Fori(0, B) as b:
                def chunk_copy(done, src_bank):
                    act.activation(chunkT, ps[:, src_bank:src_bank + 2, :], ACT.Copy).then_inc(done, 1)

                with act.Fori(0, NCH) as c:
                    act.wait_ge(yp_ready, b * 2 * NCH)
                    act.wait_ge(n_ready, (b * 2 * NCH) * TPC)
                    act.wait_ge(wT_read, 3)
                    k = b * NCH + c
                    act.wait_ge(x_tr, (b * 2 * NCH + c + 1) * TPC)
                    act.wait_ge(qk_ready, k * 4)
                    chunk_copy(xT_ready, 0)
                    act.wait_ge(k_split, k * K_STEPS)
                    for s in (2, 3):
                        act.wait_ge(qk_ready, k * 4 + s + 1)
                        act.activation(qk32[:, s, :], bank(2 + s), ACT.Identity,
                                       bias=qk_bias[:, s:s + 1]).then_inc(k32_ready, 1)

                def exps(mode, h, qp):
                    it = h * 2 + qp
                    n_min = 8 if mode == "A" else 1
                    start = filled_before(b, mode) + it * per_body(mode)
                    mins = mins_before(b, mode) + it * n_min * N_BODY
                    i = m = 0
                    for par in range(2):
                        for jj in range(UNITS):
                            u, ai = par * UNITS + jj, 0
                            for item in ring_items(UNIT[mode]):
                                tile = tile_ap(i % RING[mode])
                                if item == "A":
                                    m += 1
                                    act.wait_ge(min_ready, mins + m)
                                    where = (slice(None), ai % HALF, TPC * jj + ai // HALF, ds(it * 2 + par, 1))
                                    act.activation(tile, tile, ACT.Exp, bias=nmax[where], scale=-1.0,
                                                   accum_out=esum[where]).then_inc(tile_read, 1)
                                    ai += 1
                                elif item[0] == "F":
                                    f = int(item[1])
                                    if f == 0:
                                        m += 1
                                        act.wait_ge(min_ready, mins + m)
                                    act.activation(probs[:, f * TILE:(f + 1) * TILE], tile, ACT.Exp,
                                                   bias=fnmax[:, :], scale=-1.0).then_inc(tile_read, 1)
                                else:
                                    f = int(item[1])
                                    act.wait_ge(filled, start + i + 1)
                                    act.wait_ge(pv_done, (b * FH * NT + it * N_BODY + u) * 2)
                                    act.activation(probsT[:, f, :], tile, ACT.Copy).then_inc(tile_read, 1)
                                i += 1

                with act.Fori(0, FH) as h:
                    with act.Fori(0, 2) as qp:
                        exps("A", h, qp)

                act.wait_ge(comb, b * COMB_STEPS + 2)
                act.activation(stats32[:, 1:3, :], stats32[:, 1:3, :], ACT.Exp).then_inc(comb_e, 1)

                def roots(n):
                    act.wait_ge(ln, n * LN_STEPS + 1)
                    act.activation(rstd[:, :], var[:, :], ACT.Sqrt).then_inc(ln_sq, 1)

                with act.Fori(0, NCH) as c:
                    k = b * 2 * NCH + c
                    act.wait_ge(x_tr, (k + NCH + 1) * TPC)
                    act.wait_ge(yp_ready, k)
                    chunk_copy(xT_ready, 0)
                    act.wait_ge(o1_tr, k + 1)
                    act.wait_ge(v_ready, b * NCH + c + 1)
                    chunk_copy(o1T_ready, 4)
                roots(b * 2)
                with act.Fori(0, NCH) as c:
                    act.wait_ge(x1_tr, b * NCH + c + 1)
                    act.activation(x1T[:, :, ds(c * CH, CH)], ps[:, 0:2, :], ACT.Copy).then_inc(x1T_ready, 1)
                act.wait_ge(rt, b * ROUTE_STEPS + 3)
                act.activation(route[:, NR:2 * NR], route[:, 0:NR], ACT.Exp, bias=route[:, 48:49],
                               accum_out=route[:, 49:50]).then_inc(rt_e, 1)
                with act.Fori(0, FH) as h:
                    act.wait_ge(n_ready, (b * 2 * NCH + NCH) * TPC)
                    with act.Fori(0, 2) as qp:
                        exps("F", h, qp)
                with act.Fori(0, NCH) as c:
                    act.wait_ge(fsp, (b + 1) * PROJ)
                    k = (b * 2 + 1) * NCH + c
                    act.wait_ge(o1_tr, k + 1)
                    act.wait_ge(yp_ready, k)
                    chunk_copy(o1T_ready, 4)
                roots(b * 2 + 1)

        @block.vector
        def _(dve):
            v_b_in = b_in_rows[:, :].rearrange("p (h c i) -> p c h i", h=AH, c=3)
            dve.wait_ge(const_in, 16 * N_CONST)
            for c in range(2):
                last = dve.tensor_copy(buf_c[0:1, c * D:(c + 1) * D].rearrange("p (h i) -> p h i", h=AH),
                                       v_b_in[0:1, c, :, :])
            last.then_inc(wT_read, 1)
            dve.wait_ge(wT_ready, 1)
            for cc in range(KC):
                nat = ps[:, 2 * cc:2 * cc + 2, :].rearrange("p a n -> p (a n)")[:, 0:3 * D].rearrange(
                    "p (h c i) -> p c h i", h=AH, c=3)
                for c in range(3):
                    dve.tensor_copy(w_inT[:, cc, c * D:(c + 1) * D].rearrange("p (h i) -> p h i", h=AH),
                                    nat[:, c, :, :])
                last = dve.tensor_copy(w_outT[:, cc, :], ps[:, 4 + cc, 0:D])
            last.then_inc(wT_read, 1)
            dve.wait_ge(wT_ready, 2)
            dve.tensor_copy(qk_bias[:, :], ps[:, 6, 0:4]).then_inc(wT_read, 1)
            dve.wait_ge(wT_read, 3)

            with dve.Fori(0, B) as b:
                with dve.Fori(0, NCH) as c:
                    k = b * NCH + c
                    level = lambda lv: split[:, 0, :, lv, ds(c * CH, CH)]
                    queries, rest = qk32[:, 0:2, :], rest32[:, 0:2, :]
                    dve.wait_ge(qk_ready, k * 4 + 2)
                    dve.wait_ge(q_split, k * Q_STEPS)
                    for s in range(2):
                        last = dve.tensor_scalar(qk32[:, s, :], bank(2 + s), qk_bias[:, s:s + 1],
                                                 -float(AD) ** -0.5, ALU.add, ALU.mult)
                    last.then_inc(q32_ready, 1)
                    dve.wait_ge(q32_ready, k + 1)
                    dve.tensor_copy(level(0), queries).then_inc(q_split, 1)
                    dve.wait_ge(q_split, k * Q_STEPS + 1)
                    dve.tensor_tensor(rest, queries, level(0), ALU.subtract).then_inc(q_split, 1)
                    dve.wait_ge(q_split, k * Q_STEPS + 2)
                    dve.tensor_copy(level(1), rest).then_inc(q_split, 1)
                    dve.wait_ge(q_split, k * Q_STEPS + 3)
                    dve.tensor_tensor(level(2), rest, level(1), ALU.subtract).then_inc(q_split, 1)

                def minima(mode, h, qp):
                    it = h * 2 + qp
                    start = filled_before(b, mode) + it * per_body(mode)
                    units = b * FH * NT + it * N_BODY
                    i = 0
                    for par in range(2):
                        for jj in range(UNITS):
                            u, ai = par * UNITS + jj, 0
                            for item in ring_items(UNIT[mode]):
                                tile = tile_ap(i % RING[mode])
                                if item[0] != "T":
                                    dve.wait_ge(filled, start + i + 1)
                                if item == "A":
                                    dve.tensor_reduce(nmax[:, ai % HALF, TPC * jj + ai // HALF, ds(it * 2 + par, 1)],
                                                      tile, AX.X, ALU.min).then_inc(min_ready, 1)
                                    ai += 1
                                elif item == "F0":
                                    dve.tensor_reduce(fmin[:, 0:1], tile, AX.X, ALU.min)
                                elif item == "F1":
                                    dve.tensor_reduce(fmin[:, 1:2], tile, AX.X, ALU.min).then_inc(fmin_ready, 1)
                                    dve.wait_ge(fmin_ready, units + u + 1)
                                    dve.tensor_reduce(fnmax[:, :], fmin[:, :], AX.X, ALU.min).then_inc(min_ready, 1)
                                i += 1
                            if mode == "F":
                                dve.wait_ge(pv_done, (units + u + 1) * 2)
                                dve.reciprocal(frec[:, :], ps[:, O_BANK, FD:FD + 1]).then_inc(o_rec, 1)
                                dve.wait_ge(o_rec, units + u + 1)
                                dve.tensor_scalar(fo[:, qp * N_BODY + u, ds(h * FD, FD)] if isinstance(qp, int) else
                                                  fo[:, ds(qp * N_BODY + u, 1), ds(h * FD, FD)],
                                                  ps[:, O_BANK, 0:FD], frec[:, :], None, ALU.mult).then_inc(o_read, 1)

                with dve.Fori(0, FH) as h:
                    with dve.Fori(0, 2) as qp:
                        minima("A", h, qp)

                n = NT * AH
                lows = nmax[:, :, :, :].rearrange("p f t a -> p f (t a)")
                sums = esum[:, :, :, :].rearrange("p f t a -> p f (t a)")
                base = b * COMB_STEPS
                dve.wait_ge(tile_read, read_before(b, "A") + A_TILES)
                dve.wait_ge(k_split, (b + 1) * NCH * K_STEPS)
                dve.tensor_tensor(stats32[:, 0, :], lows[:, 0, :], lows[:, 1, :], ALU.min).then_inc(comb, 1)
                dve.wait_ge(comb, base + 1)
                dve.tensor_tensor(stats32[:, 1:3, :], stats32[:, 0:1, :].to_broadcast([P, HALF, n]), lows,
                                  ALU.subtract).then_inc(comb, 1)
                dve.wait_ge(comb_e, b + 1)
                dve.tensor_tensor(stats32[:, 1:3, :], stats32[:, 1:3, :], sums, ALU.mult).then_inc(comb, 1)
                dve.wait_ge(comb, base + 3)
                dve.tensor_tensor(stats32[:, 3, :], stats32[:, 1, :], stats32[:, 2, :], ALU.add).then_inc(comb, 1)
                dve.wait_ge(comb, base + 4)
                dve.reciprocal(stats32[:, 4, :], stats32[:, 3, :]).then_inc(comb, 1)
                dve.wait_ge(comb, base + 5)
                dve.tensor_tensor(att[:, :, :].rearrange("p t a -> p (t a)"), stats32[:, 3, :], stats32[:, 4, :],
                                  ALU.mult).then_inc(comb, 1)
                dve.drain()

                def add_rows(k, c):
                    dve.wait_ge(yp_ready, k + 1)
                    dve.wait_ge(res_ready, k + 1)
                    for j in range(2):
                        last = dve.tensor_tensor(y[:, ds(c * TPC + 2 * j, 2), :], bank_rows(6 + j),
                                                 rows_in[:, 2 * j:2 * j + 2, :], ALU.add)
                    last.then_inc(y_ready, 1)
                    dve.drain()
                    for t in range(TPC):
                        last = dve.bn_stats(st[:, t, :], flat(y[:, ds(c * TPC + t, 1), :]))
                    last.then_inc(bn_ready, 1)
                    dve.drain()
                    for t in range(TPC):
                        last = dve.bn_aggr(mv_chunk[:, t, :], st[:, t, :])
                    last.then_inc(bn_ready, 1)
                    dve.wait_ge(bn_ready, k * BN_STEPS + 2)
                    dve.tensor_copy(mv[:, ds(c * TPC, TPC), :], mv_chunk[:, :, :]).then_inc(bn_ready, 1)
                    dve.wait_ge(bn_ready, k * BN_STEPS + 3)

                def norm_factors(n):
                    base = n * LN_STEPS
                    dve.tensor_scalar(var[:, :], mv[:, :, 1], EPS, None, ALU.add).then_inc(ln, 1)
                    dve.wait_ge(ln_sq, n + 1)
                    dve.reciprocal(rstd[:, :], rstd[:, :]).then_inc(ln, 1)
                    dve.wait_ge(ln, base + 2)
                    dve.tensor_tensor(newt[:, :], rstd[:, :], rstd[:, :], ALU.mult).then_inc(ln, 1)
                    dve.wait_ge(ln, base + 3)
                    dve.tensor_tensor(newt[:, :], newt[:, :], var[:, :], ALU.mult).then_inc(ln, 1)
                    dve.wait_ge(ln, base + 4)
                    dve.tensor_scalar(newt[:, :], newt[:, :], -0.5, 1.5, ALU.mult, ALU.add).then_inc(ln, 1)
                    dve.wait_ge(ln, base + 5)
                    dve.tensor_tensor(rstd[:, :], rstd[:, :], newt[:, :], ALU.mult).then_inc(ln, 1)
                    dve.drain()

                def norm_chunk(k, c):
                    dve.wait_ge(n_out, k * 16)
                    for t in range(TPC):
                        at = c * TPC + t
                        last = dve.tensor_scalar(rows_mid[:, t, :], flat(y[:, ds(at, 1), :]), mv[:, ds(at, 1), 0],
                                                 rstd[:, ds(at, 1)], ALU.subtract, ALU.mult)
                    last.then_inc(n_ready, TPC)

                with dve.Fori(0, NCH) as c:
                    k = b * 2 * NCH + c
                    dve.wait_ge(v_ready, b * NCH + c + 1)
                    dve.wait_ge(o1_tr, k)
                    dve.wait_ge(n_out, b * 2 * NCH * 16)
                    heads = lambda ap: ap.rearrange("p t (h i) -> p t h i", h=AH)
                    for j in range(2):
                        last = dve.tensor_tensor(heads(rows_mid[:, 2 * j:2 * j + 2, :]), heads(bank_rows(2 + j)),
                                                 v_b_in[:, 2:3, :, :].to_broadcast([P, 2, AH, AD]), ALU.add)
                    last.then_inc(v_read, 1)
                    dve.wait_ge(v_read, b * NCH + c + 1)
                    dve.tensor_tensor(heads(rows_mid), heads(rows_mid),
                                      att[:, ds(c * TPC, TPC), :].unsqueeze(3).to_broadcast([P, TPC, AH, AD]),
                                      ALU.mult).then_inc(o1_ready, 1)
                    add_rows(k, c)
                norm_factors(b * 2)
                with dve.Fori(0, NCH) as c:
                    dve.wait_ge(o1_tr, b * 2 * NCH + NCH)
                    dve.wait_ge(x1_tr, b * NCH + c)
                    norm_chunk(b * 2 * NCH + c, c)

                base = b * ROUTE_STEPS
                logits, probs_r = route[:, 0:NR], route[:, NR:2 * NR]
                best, order, low, total, rec, back = (route[:, 32:40], route[:, 40:48], route[:, 48:49],
                                                      route[:, 49:50], route[:, 50:51], route[:, 52:60])
                dve.wait_ge(x1T_ready, (b + 1) * NCH)
                dve.tensor_reduce(xsum[:, :], x1T[:, :, :], AX.X, ALU.add).then_inc(rt, 1)
                dve.wait_ge(rt_mm, b + 1)
                dve.scalar_tensor_tensor(logits, ps[0:1, 2, 0:NR], 1.0 / L, br_row[:, :],
                                         ALU.mult, ALU.add).then_inc(rt, 1)
                dve.wait_ge(rt, base + 2)
                dve.tensor_reduce(low, logits, AX.X, ALU.max, negate=True).then_inc(rt, 1)
                dve.wait_ge(rt_e, b + 1)
                dve.reciprocal(rec, total).then_inc(rt, 1)
                dve.wait_ge(rt, base + 4)
                dve.tensor_scalar(probs_r, probs_r, rec, None, ALU.mult).then_inc(rt, 1)
                dve.drain()
                dve.max(best, probs_r).then_inc(rt, 1)
                dve.drain()
                dve.max_index(top_i[:, :], best, probs_r).then_inc(rt, 1)
                dve.wait_ge(rt, base + 7)
                dve.tensor_copy(order, top_i[:, :]).then_inc(rt, 1)
                dve.wait_ge(rt, base + 8)
                dve.memset(order[:, FH:8], -float(NR))
                dve.tensor_scalar(order[:, 0:FH], order[:, 0:FH], -1.0, None, ALU.mult).then_inc(rt, 1)
                dve.drain()
                dve.max(back, order).then_inc(rt, 1)
                dve.wait_ge(rt, base + 10)
                dve.tensor_scalar(head_i[:, :], back, -1.0, None, ALU.mult).then_inc(rt, 1)

                with dve.Fori(0, NCH) as c:
                    dve.wait_ge(wv_in, (b + 1) * 2 * FH * 16)
                    dve.wait_ge(fv_ready, b * NCH + c + 1)
                    for t in range(TPC):
                        last = dve.tensor_tensor(
                            vals[:, ds(c * TPC + t, 1), :, 0:FD].rearrange("p a h n -> p (a h) n"),
                            ps[:, 4 + t // 2, (t % 2) * D:(t % 2 + 1) * D].rearrange("p (h n) -> p h n", h=FH),
                            bv_sel[:, :].rearrange("p (h n) -> p h n", h=FH), ALU.add)
                    last.then_inc(fv_read, 1)

                def read_head(hh):
                    with dve.Fori(0, NCH) as c:
                        k = b * PROJ + hh * NCH + c
                        dve.wait_ge(fsp, k)
                        for s in range(2):
                            dve.wait_ge(fp_ready, k * 2 + s + 1)
                            dve.tensor_scalar(f32s[:, s, :], bank(FP_BANK), bqk_sel[:, s:s + 1],
                                              -float(FD) ** -0.5 if s == 0 else 1.0,
                                              ALU.add, ALU.mult).then_inc(fp_read, 1)
                read_head(0)
                with dve.Fori(0, FH) as h:
                    read_head(h + 1)
                    with dve.Fori(0, 2) as qp:
                        minima("F", h, qp)

                with dve.Fori(0, NCH) as c:
                    add_rows((b * 2 + 1) * NCH + c, c)
                norm_factors(b * 2 + 1)
                with dve.Fori(0, NCH) as c:
                    dve.wait_ge(o1_tr, (b + 1) * 2 * NCH)
                    norm_chunk((b * 2 + 1) * NCH + c, c)


_INS = ["x", "w_in", "b_in", "w_out", "b_out"]
_ALL = ["L0_attn_" + n for n in _INS] + ["L0_ffn_" + n for n in
                                         ("Wq", "bq", "Wk", "bk", "Wv", "bv", "Wr", "br", "Wo", "bo")]


def kernel(**inputs):
    import numpy as _np
    import concourse.bacc as _bacc
    from concourse import mybir as _mybir
    from concourse.bass_utils import run_bass_kernel_spmd as _run

    nc = _bacc.Bacc("TRN2", target_bir_lowering=False, num_devices=1)
    arrays, args = {}, []
    for name in _ALL:
        a = _np.ascontiguousarray(inputs[name])
        arrays[f"in_{name}"] = a
        args.append(nc.dram_tensor(f"in_{name}", a.shape, _mybir.dt.from_np(a.dtype), kind="ExternalInput").ap())
    out = nc.dram_tensor("out_rows", (B, L, D), _mybir.dt.float32, kind="ExternalOutput").ap()
    build(nc, *args, out)
    r = _run(nc, [arrays], core_ids=[0])
    return r.results[0]["out_rows"]
```

```python
import concourse.bass as bass
from concourse import mybir
from contextlib import ExitStack

F32 = mybir.dt.float32
BF16 = mybir.dt.bfloat16
U32 = mybir.dt.uint32
I32 = mybir.dt.int32
ALU = mybir.AluOpType
ACT = mybir.ActivationFunctionType
AX = mybir.AxisListType
ds = bass.ds

P = 128
B, L, D = 4, 2048, 256
NT = L // P
KC = D // P
CH = 512
NCH = L // CH
TPC = CH // P
AH, AD = 16, D // 16
GH = P // AD
FH, FD = 4, 64
NR = 16
LV = 3
Q_LEVEL = (0, 0, 0, 1, 1, 2)
K_LEVEL = (0, 1, 2, 0, 1, 0)
SK = len(Q_LEVEL) * AD
TILE = 1024
HALF = L // TILE
EPS = 1e-5
SLOTS = 3
A_SLOTS = 4
UNITS = 4
CREDIT = A_SLOTS


def schedule(mode):
    pe, act, dve = [], [], []
    units = range(2 * UNITS)
    if mode == "A":
        pe = [("A", u, i) for u in units for i in range(8)]
        return pe, pe, pe
    if mode == "AF":
        for u in units:
            A = lambda *i: [("A", u, n) for n in i]
            proj = u % UNITS == 0
            F, T = [("F", u, 0), ("F", u, 1)], [("T", u, 0), ("T", u, 1)]
            P0, P1 = [("P", u, 0)] * proj, [("P", u, 1)] * proj
            pe += A(0) + F + P0 + A(1, 2) + P1 + T[:1] + A(3) + T[1:] + A(4) + [("PV", u, 0)] \
                + A(5, 6, 7) + [("PV", u, 1)]
            act += A(0) + F + A(1, 2) + T[:1] + A(3) + T[1:] + A(4, 5, 6, 7)
            dve += A(0) + F + P0 + A(1, 2) + P1 + A(3, 4, 5, 6, 7) + [("O", u, 0)]
        return pe, act, dve
    F = lambda u: [("F", u, 0), ("F", u, 1)] * (u < 2 * UNITS)
    T = lambda u: [("T", u, 0), ("T", u, 1)]
    P = lambda u, i: [("P", u, i)] * (u % UNITS == 0)
    pe += F(0)
    act += F(0)
    dve += F(0)
    for u in units:
        pe += F(u + 1) + T(u) + P(u, 0) + [("PV", u, 0), ("PV", u, 1)] + P(u, 1)
        act += T(u) + F(u + 1)
        dve += F(u + 1) + P(u, 0) + P(u, 1) + [("O", u, 0)]
    return pe, act, dve


def slot_of(mode, tile, n):
    if mode == "F":
        return {"F": tile[2], "T": 2}[tile[0]]
    return n % (A_SLOTS if mode == "A" else SLOTS)


def build(nc, x, w_in, b_in, w_out, b_out, wq, bq, wk, bk, wv, bv, wr, br, wo, bo, out):
    ctx = ExitStack()
    with ctx:
        sb = lambda name, shape, dt=F32: ctx.enter_context(nc.sbuf_tensor(name, shape, dt))
        sem = lambda name: ctx.enter_context(nc.semaphore(name))
        ctx.enter_context(nc.allow_non_contiguous_dma(reason="bias columns"))

        x1_dram = nc.dram_tensor("x1_rows", [NT, P, D], F32).ap()
        ident = sb("ident", [P, P])
        w_inT = sb("w_inT", [P, KC, 3 * D])
        w_outT = sb("w_outT", [P, KC, D])
        wo_sb = sb("wo_sb", [P, KC, D])
        wr_sb = sb("wr_sb", [P, KC, NR])
        b_in_rows = sb("b_in_rows", [P, 3 * D])
        b_out_rows = sb("b_out_rows", [P, D])
        bo_rows = sb("bo_rows", [P, D])
        br_row = sb("br_row", [1, NR])
        qk_bias = sb("qk_bias", [P, 4])
        wv_sel = sb("wv_sel", [P, KC, FH * FD])
        bv_sel = sb("bv_sel", [P, FH * FD])
        wqk_sel = sb("wqk_sel", [P, KC, 2, 2 * FD])
        bqk_sel = sb("bqk_sel", [P, 2])
        one = sb("one", [1, 1])

        split = sb("split", [P, 2, 2, LV, L], BF16)
        stack = sb("stack", [P, 2, 2, L], BF16)
        fq = sb("fq", [P, 2, 3, L], BF16)
        fk = sb("fk", [P, 2, 2, L], BF16)
        vals = sb("vals", [P, NT, FH, FD + 1])
        x1T = sb("x1T", [P, KC, L])
        fo = sb("fo", [P, NT, FH * FD])
        shared = sb("shared", [P, 2 * L])
        probs = shared[:, 0:L]
        probsT = shared[:, L:2 * L].rearrange("p (f k) -> p f k", f=HALF)
        y = shared[:, :].rearrange("p (t d) -> p t d", t=NT)
        qk32 = shared[:, 0:L].rearrange("p (s n) -> p s n", s=4)
        rest32 = shared[:, L:2 * L].rearrange("p (s n) -> p s n", s=4)
        w_rows = shared[:, 0:6 * D].rearrange("p (t d) -> p t d", t=6)
        w_out_rows = shared[:, 6 * D:8 * D].rearrange("p (t d) -> p t d", t=KC)
        stats32 = shared[:, 0:6 * NT * AH].rearrange("p (s n) -> p s n", s=6)
        buf_a = sb("buf_a", [P, TPC * D])
        buf_b = sb("buf_b", [P, TPC * D])
        buf_c = sb("buf_c", [P, TPC * D])
        rows_in = buf_a[:, :].rearrange("p (t d) -> p t d", t=TPC)
        chunkT = buf_b[:, :].rearrange("p (c n) -> p c n", c=KC)
        rows_mid = buf_c[:, :].rearrange("p (t d) -> p t d", t=TPC)
        f32s = buf_a[:, :].rearrange("p (s n) -> p s n", s=2)
        frest = buf_b[:, :].rearrange("p (s n) -> p s n", s=2)
        fmid = buf_c[:, 0:CH // 2].bitcast(BF16)

        nmax = sb("nmax", [P, HALF, NT, AH])
        esum = sb("esum", [P, HALF, NT, AH])
        att = sb("att", [P, NT, AH])
        fmin = sb("fmin", [P, HALF])
        fnmax = sb("fnmax", [P, 1])
        frec = sb("frec", [P, 1])
        mv = sb("mv", [P, NT, 2])
        st = sb("st", [P, TPC, 6])
        mv_chunk = sb("mv_chunk", [P, TPC, 2])
        var = sb("var", [P, NT])
        rstd = sb("rstd", [P, NT])
        newt = sb("newt", [P, NT])
        xsum = sb("xsum", [P, KC])
        route = sb("route", [1, 4 * NR])
        top_i = sb("top_i", [1, 8], U32)
        head_i = sb("head_i", [1, 8], I32)

        ps = ctx.enter_context(nc.psum_tensor("ps", [P, 8, CH], F32))
        O_BANK, FP_BANK = 6, 7
        bank = lambda n: ps[:, n, :]
        bank_rows = lambda n: ps[:, n, :].rearrange("p (t d) -> p t d", d=D)

        const_in = sem("const_in")
        const_made = sem("const_made")
        wT_ready = sem("wT_ready")
        wT_read = sem("wT_read")
        x_in = sem("x_in")
        x_tr = sem("x_tr")
        xT_ready = sem("xT_ready")
        qk_ready = sem("qk_ready")
        q32_ready = sem("q32_ready")
        k32_ready = sem("k32_ready")
        q_split = sem("q_split")
        k_split = sem("k_split")
        stack_in = [sem("stack_in_even"), sem("stack_in_odd")]
        filled = sem("filled")
        min_ready = sem("min_ready")
        fmin_ready = sem("fmin_ready")
        tile_read = sem("tile_read")
        pv_done = sem("pv_done")
        o_rec = sem("o_rec")
        o_read = sem("o_read")
        comb = sem("comb")
        comb_e = sem("comb_e")
        v_ready = sem("v_ready")
        v_read = sem("v_read")
        o1_ready = sem("o1_ready")
        o1_tr = sem("o1_tr")
        o1T_ready = sem("o1T_ready")
        res_in = sem("res_in")
        res_ready = sem("res_ready")
        yp_ready = sem("yp_ready")
        y_ready = sem("y_ready")
        bn_ready = sem("bn_ready")
        ln = sem("ln")
        ln_sq = sem("ln_sq")
        n_ready = sem("n_ready")
        n_out = sem("n_out")
        x1_tr = sem("x1_tr")
        x1T_ready = sem("x1T_ready")
        rt = sem("rt")
        rt_mm = sem("rt_mm")
        rt_e = sem("rt_e")
        wv_in = sem("wv_in")
        fv_ready = sem("fv_ready")
        fv_read = sem("fv_read")
        fpw_in = sem("fpw_in")
        fp_ready = sem("fp_ready")
        fp_read = sem("fp_read")
        fsp = sem("fsp")
        fo_stage = sem("fo_stage")

        N_BODY = 2 * UNITS
        BODIES = FH * 2
        Q_STEPS = K_STEPS = 4
        LN_STEPS, BN_STEPS = 6, 3
        COMB_STEPS = 6
        ROUTE_STEPS = 11
        N_CONST = 8
        HEAD_DMAS = 12
        SEL_DMAS = 8
        PROJ = (FH + 1) * NCH

        class Phase:
            def __init__(self, mode):
                self.mode = mode
                self.pe, self.act, self.dve = schedule(mode)
                self.fills = [t for t in self.pe if t[0] in "AFT"]
                self.reads = [t for t in self.act if t[0] in "AFT"]
                self.tiles = len(self.fills)
                self.mins = [t for t in self.dve if t[0] == "A" or t[0] == "F" and t[2] == 1]
                self.slot = {t: slot_of(mode, t, n) for n, t in enumerate(self.fills)}
                self.fill_no = {t: n + 1 for n, t in enumerate(self.fills)}
                self.read_no = {t: n + 1 for n, t in enumerate(self.reads)}
                self.min_no = {t: n + 1 for n, t in enumerate(self.mins)}

            def before(self, tile):
                n = self.fill_no[tile] - 1
                for j in range(n - 1, -1, -1):
                    if self.slot[self.fills[j]] == self.slot[tile]:
                        return self.read_no[self.fills[j]]
                return max(self.read_no[t] for t in self.fills if self.slot[t] == self.slot[tile]) - self.tiles

        PA, PAF, PF = Phase("A"), Phase("AF"), Phase("F")

        def filled_before(b):
            return 0 if b is None else BODIES * (PA.tiles + PAF.tiles * b)

        def mins_before(b):
            return 0 if b is None else BODIES * (len(PA.mins) + len(PAF.mins) * b)

        def flat(ap):
            return ap.rearrange("p a n -> p (a n)")

        def ring(slot):
            return flat(ps[:, 2 * slot:2 * slot + 2, :])

        def next_batches(eng, step):
            with eng.Fori(0, B - 1) as b:
                step(b, PAF)
            step(B - 1, PF)

        block = ctx.enter_context(nc.Block())

        @block.sync
        def _(sp):
            row = lambda v: v.rearrange("(a n) -> a n", a=1)
            sp.dma_start(w_rows, w_in.rearrange("(t p) d -> p t d", p=P)).then_inc(const_in, 16)
            sp.dma_start(w_out_rows, w_out.rearrange("(t p) d -> p t d", p=P)).then_inc(const_in, 16)
            sp.dma_start(wo_sb[:, :, :], wo.rearrange("(c p) n -> p c n", p=P)).then_inc(const_in, 16)
            sp.dma_start(wr_sb[:, :, :], wr.rearrange("(c p) n -> p c n", p=P)).then_inc(const_in, 16)
            sp.dma_start(b_in_rows[:, :], b_in.partition_broadcast(P)).then_inc(const_in, 16)
            sp.dma_start(b_out_rows[:, :], b_out.partition_broadcast(P)).then_inc(const_in, 16)
            sp.dma_start(bo_rows[:, :], bo.partition_broadcast(P)).then_inc(const_in, 16)
            sp.dma_start(br_row[:, :], row(br)).then_inc(const_in, 16)

            x_rows = x.rearrange("b (t p) d -> (b t) p d", p=P)
            out_tiles = out.rearrange("b (t p) d -> (b t) p d", p=P)

            def load_x(b, phase, after=True):
                with sp.Fori(0, NCH) as c:
                    sp.wait_ge(y_ready, b * 2 * NCH + c if phase else (b * 2 - 1) * NCH if after else 0)
                    sp.wait_ge(x_tr, (b * 2 * NCH + phase * NCH + c) * TPC)
                    sp.dma_start(rows_in, x_rows[ds((b * NCH + c) * TPC, TPC), :, :].rearrange("t p d -> p t d")
                                 ).then_inc(x_in, 16)

            def stack_heads(b, before, tiles, load_head=None):
                with sp.Fori(0, 2) as hh:
                    sp.wait_ge(q_split, (b + 1) * NCH * Q_STEPS)
                    sp.wait_ge(k_split, (b + 1) * NCH * K_STEPS)
                    for r in range(GH):
                        sp.wait_ge(filled, before + (hh * (GH - 1) * tiles if r == 0 else (hh * GH + r - 1) * tiles))
                        for side, levels in ((0, Q_LEVEL), (1, K_LEVEL)):
                            for g, lv in enumerate(levels):
                                sp.dma_start(stack[g * AD:(g + 1) * AD, r % 2, side, :],
                                             flat(split[r * AD:(r + 1) * AD, side, ds(hh, 1), lv, :])
                                             ).then_inc(stack_in[r % 2], 16)
                        if load_head and r % UNITS == 0:
                            load_head(hh * 2 + r // UNITS + 1)

            load_x(0, 0, False)
            stack_heads(0, 0, PA.tiles // 2)

            def step(b, phase):
                load_x(b, 1)
                with sp.Fori(0, NCH) as c:
                    k = b * 2 * NCH + c
                    sp.wait_ge(n_out, k * 16)
                    sp.wait_ge(n_ready, (k + 1) * TPC)
                    sp.dma_start(x1_dram[ds((c + 1) * TPC - TPC, TPC), :, :].rearrange("t p d -> p t d"),
                                 rows_mid).then_inc(n_out, 16)
                if phase is PAF:
                    load_x(b + 1, 0)
                with sp.Fori(0, FH) as h:
                    sp.wait_ge(rt, (b + 1) * ROUTE_STEPS)
                    i = sp.value_load(head_i[0:1, ds(h % FH, 1)], min_val=0, max_val=NR - 1)
                    sp.dma_start(wv_sel[:, :, ds(h * FD, FD)],
                                 wv[:, ds(i * FD, FD)].rearrange("(c p) n -> p c n", p=P)).then_inc(wv_in, 16)
                    sp.dma_start(bv_sel[:, ds(h * FD, FD)],
                                 bv[ds(i * FD, FD)].partition_broadcast(P)).then_inc(wv_in, 16)

                def load_head(hh):
                    done = (b * PROJ + hh * NCH) * 2
                    i = sp.value_load(head_i[0:1, ds(hh % FH, 1)], min_val=0, max_val=NR - 1)
                    sp.wait_ge(fp_ready, done)
                    sp.wait_ge(fp_read, done)
                    for s, (w, bias) in enumerate(((wq, bq), (wk, bk))):
                        for twice in range(2):
                            sp.dma_start(wqk_sel[:, :, s, twice * FD:(twice + 1) * FD],
                                         w[:, ds(i * FD, FD)].rearrange("(c p) n -> p c n", p=P)).then_inc(fpw_in, 16)
                            sp.dma_start(bqk_sel[twice * FD:(twice + 1) * FD, s:s + 1],
                                         bias[ds(i * FD, FD)].rearrange("(p a) -> p a", a=1)).then_inc(fpw_in, 16)

                with sp.Fori(0, 1 if phase is PAF else FH + 1) as hh:
                    load_head(hh)
                if phase is PAF:
                    stack_heads(b + 1, filled_before(b), PAF.tiles // 2, load_head)

                with sp.Fori(0, NCH) as c:
                    sp.wait_ge(fsp, (b + 1) * PROJ)
                    sp.wait_ge(y_ready, (b * 2 + 1) * NCH + c)
                    sp.dma_start(rows_in, x1_dram[ds(c * TPC, TPC), :, :].rearrange("t p d -> p t d")
                                 ).then_inc(res_in, 16)
                with sp.Fori(0, NCH) as c:
                    k = (b * 2 + 1) * NCH + c
                    sp.wait_ge(n_out, k * 16)
                    sp.wait_ge(n_ready, (k + 1) * TPC)
                    sp.dma_start(out_tiles[ds((b * NCH + c) * TPC, TPC), :, :].rearrange("t p d -> p t d"),
                                 rows_mid).then_inc(n_out, 16)
            next_batches(sp, step)
            sp.wait_ge(n_out, B * 2 * NCH * 16)

        @block.gpsimd
        def _(pool):
            pool.memset(ident[:, :], 0.0).then_inc(const_made, 1)
            pool.memset(one[:, :], 1.0).then_inc(const_made, 1)
            pool.memset(vals[:, :, :, FD:FD + 1], 1.0).then_inc(const_made, 1)
            pool.wait_ge(const_made, 3)
            pool.affine_select(out=ident[:, :], in_=ident[:, :], compare_op=ALU.not_equal, fill=1.0, base=0,
                               pattern=[[-1, P]], channel_multiplier=1).then_inc(const_made, 1)
            def split_keys(b, used):
                with pool.Fori(0, NCH) as c:
                    pool.wait_ge(const_in, 16 * N_CONST)
                    pool.wait_ge(filled, used)
                    k = b * NCH + c
                    level = lambda lv: split[:, 1, :, lv, ds(c * CH, CH)]
                    keys, rest = qk32[:, 2:4, :], rest32[:, 2:4, :]
                    pool.wait_ge(k32_ready, k * 2 + 2)
                    pool.tensor_copy(level(0), keys).then_inc(k_split, 1)
                    pool.drain()
                    pool.tensor_tensor(rest, keys, level(0), ALU.subtract).then_inc(k_split, 1)
                    pool.drain()
                    pool.tensor_copy(level(1), rest).then_inc(k_split, 1)
                    pool.drain()
                    pool.tensor_tensor(level(2), rest, level(1), ALU.subtract).then_inc(k_split, 1)

            split_keys(0, 0)

            def step(b, phase):
                with pool.Fori(0, NCH) as c:
                    pool.wait_ge(x_tr, (b * 2 * NCH + NCH + c + 1) * TPC)
                    pool.tensor_tensor(rows_in, rows_in, b_out_rows[:, :].unsqueeze(1).to_broadcast([P, TPC, D]),
                                       ALU.add).then_inc(res_ready, 1)
                if phase is PAF:
                    split_keys(b + 1, filled_before(b))
                def split_head(hh, par):
                    with pool.Fori(0, NCH) as c:
                        k = b * PROJ + hh * NCH + c
                        H = P // 2
                        low, high, every = (0, H), (H, P), (0, P)
                        q_to = lambda i, r: flat(fq[r[0]:r[1], ds(par, 1), i, ds(c * CH, CH)])
                        k_to = lambda i, r: flat(fk[r[0]:r[1], ds(par, 1), i, ds(c * CH, CH)])
                        q32, k32 = (lambda r: f32s[r[0]:r[1], 0, :]), (lambda r: f32s[r[0]:r[1], 1, :])
                        qr, kr = (lambda r: frest[r[0]:r[1], 0, :]), (lambda r: frest[r[0]:r[1], 1, :])
                        pool.wait_ge(fp_read, k * 2 + 2)
                        pool.wait_ge(filled, filled_before(b) + (hh - 1) * 2 * phase.tiles)
                        pool.tensor_copy(q_to(0, every), q32(every))
                        pool.drain()
                        pool.tensor_tensor(qr(every), q32(every), q_to(0, every), ALU.subtract)
                        pool.drain()
                        pool.tensor_copy(q_to(1, every), qr(every))
                        pool.drain()
                        pool.tensor_copy(q_to(2, low), q32(low))
                        pool.tensor_copy(k_to(0, low), k32(low))
                        pool.drain()
                        pool.tensor_tensor(kr(low), k32(low), k_to(0, low), ALU.subtract)
                        pool.drain()
                        pool.tensor_copy(fmid[0:H, :], kr(low))
                        pool.drain()
                        pool.tensor_tensor(k_to(1, low), kr(low), fmid[0:H, :], ALU.subtract)
                        pool.drain()
                        pool.tensor_copy(k_to(1, high), k32(high))
                        pool.tensor_tensor(q_to(2, high), qr(high), q_to(1, high), ALU.subtract)
                        pool.drain()
                        pool.tensor_tensor(kr(high), k32(high), k_to(1, high), ALU.subtract)
                        pool.drain()
                        pool.tensor_copy(k_to(0, high), kr(high)).then_inc(fsp, 1)
                        pool.drain()
                with pool.Fori(0, FH) as h:
                    split_head(h + 1, (h + 1) % 2)
                with pool.Fori(0, NCH) as c:
                    pool.wait_ge(o_read, (b + 1) * FH * NT)
                    k = (b * 2 + 1) * NCH + c
                    pool.wait_ge(o1_tr, k)
                    pool.tensor_copy(rows_mid, fo[:, ds(c * TPC, TPC), :]).then_inc(fo_stage, 1)
                    pool.wait_ge(res_in, (b * NCH + c + 1) * 16)
                    pool.tensor_tensor(rows_in, rows_in, bo_rows[:, :].unsqueeze(1).to_broadcast([P, TPC, D]),
                                       ALU.add).then_inc(res_ready, 1)

            next_batches(pool, step)

        @block.tensor
        def _(pe):
            pe.wait_ge(const_made, 4)
            pe.wait_ge(const_in, 16 * N_CONST)
            for cc in range(KC):
                for t in range(6):
                    col = cc * 2 * CH + t * P
                    pe.transpose(ps[:, col // CH, col % CH:col % CH + P],
                                 w_rows[:, t, cc * P:(cc + 1) * P], ident[:, :])
                for t in range(KC):
                    last = pe.transpose(ps[:, 4 + cc, t * P:(t + 1) * P],
                                        w_out_rows[:, t, cc * P:(cc + 1) * P], ident[:, :])
            last.then_inc(wT_ready, 1)
            pe.wait_ge(wT_read, 1)
            for s in range(4):
                last = pe.matmul(ps[:, 6, s:s + 1], buf_c[0:1, s * P:(s + 1) * P], one[:, :],
                                 start=True, stop=True)
            last.then_inc(wT_ready, 1)
            pe.wait_ge(wT_read, 2)

            def transpose_x(k):
                pe.wait_ge(x_in, (k + 1) * 16)
                for cc in range(KC):
                    for t in range(TPC):
                        last = pe.transpose(ps[:, cc, t * P:(t + 1) * P],
                                            rows_in[:, t, cc * P:(cc + 1) * P], ident[:, :])
                last.then_inc(x_tr, TPC)
                pe.wait_ge(xT_ready, k + 1)

            def project_rows(done, w, bank0, rowsT=chunkT):
                for t in range(TPC):
                    for cc in range(KC):
                        last = pe.matmul(ps[:, bank0 + t // 2, (t % 2) * D:(t % 2 + 1) * D],
                                         rowsT[:, cc, t * P:(t + 1) * P], w[:, cc, :],
                                         start=(cc == 0), stop=(cc == KC - 1))
                last.then_inc(done, 1)

            def transpose_rows(done, bank0):
                for cc in range(KC):
                    for t in range(TPC):
                        last = pe.transpose(ps[:, bank0 + cc, t * P:(t + 1) * P],
                                            rows_mid[:, t, cc * P:(cc + 1) * P], ident[:, :])
                last.then_inc(done, 1)

            def queries_keys(b, free):
                with pe.Fori(0, NCH) as c:
                    k = b * NCH + c
                    for what, count in free:
                        pe.wait_ge(what, count)
                    transpose_x(b * 2 * NCH + c)
                    pe.wait_ge(q32_ready, k)
                    pe.wait_ge(k32_ready, k * 2)
                    for s in range(4):
                        for cc in range(KC):
                            last = pe.matmul(bank(2 + s), w_inT[:, cc, s * P:(s + 1) * P], chunkT[:, cc, :],
                                             start=(cc == 0), stop=(cc == KC - 1))
                        last.then_inc(qk_ready, 1)

            def scores(phase, b, h, qp):
                it = h * 2 + qp
                ab = 0 if b is None else b + 1
                start = filled_before(b) + CREDIT + it * phase.tiles
                if phase is not PF:
                    pe.wait_ge(q32_ready, (ab + 1) * NCH)
                    pe.wait_ge(k32_ready, (ab + 1) * NCH * 2)
                if phase is not PA:
                    pe.wait_ge(fv_read, (b + 1) * NCH)
                    pe.wait_ge(fsp, b * PROJ + (h + 1) * NCH)
                for tile in phase.pe:
                    kind, u, n = tile
                    par, jj = u // UNITS, u % UNITS
                    if kind == "PV":
                        pe.wait_ge(tile_read, start + phase.read_no["T", u, n])
                        if n == 0:
                            pe.wait_ge(o_read, b * FH * NT + it * N_BODY + u)
                        for kt in range(NT // 2):
                            last = pe.matmul(
                                ps[:, O_BANK, 0:FD + 1], probsT[:, n, kt * P:(kt + 1) * P],
                                flat(vals[:, n * (NT // 2) + kt, ds(h, 1), :]),
                                start=(n == 0 and kt == 0), stop=(n == 1 and kt == NT // 2 - 1))
                        last.then_inc(pv_done, 1)
                        continue
                    if kind == "P":
                        project_chunk(b, h + 1, qp * 2 + par, n)
                        continue
                    slot = phase.slot[tile]
                    pe.wait_ge(tile_read, start + phase.before(tile))
                    if kind == "T" and n == 0:
                        pe.wait_ge(tile_read, start + phase.read_no["F", u, 1])
                    if kind == "A" and n == jj == 0:
                        pe.wait_ge(stack_in[par], (ab * BODIES + it + 1) * HEAD_DMAS * 16)
                    for j in range(2):
                        dst = 2 * slot + j
                        if kind == "A":
                            t, col = TPC * jj + n // HALF, (n % HALF) * TILE + j * CH
                            last = pe.matmul(bank(dst), stack[0:SK, par, 0, t * P:(t + 1) * P],
                                             stack[0:SK, par, 1, col:col + CH], start=True, stop=True)
                        elif kind == "F":
                            col = n * TILE + j * CH
                            for s in range(3):
                                last = pe.matmul(bank(dst), flat(fq[:, ds(h % 2, 1), s, ds(qp * TILE + u * P, P)]),
                                                 flat(fk[:, ds(h % 2, 1), s // 2, col:col + CH]),
                                                 start=(s == 0), stop=(s == 2))
                        else:
                            col = n * TILE + j * CH
                            for kt in range(TPC):
                                last = pe.transpose(ps[:, dst, kt * P:(kt + 1) * P],
                                                    probs[:, col + kt * P:col + (kt + 1) * P], ident[:, :])
                    last.then_inc(filled, 1)

            def project_chunk(b, hh, c, s):
                k = b * PROJ + hh * NCH + c
                pe.wait_ge(fpw_in, (b * (FH + 1) + hh + 1) * SEL_DMAS * 16)
                pe.wait_ge(fp_read, k * 2 + s)
                for cc in range(KC):
                    last = pe.matmul(bank(FP_BANK), wqk_sel[:, cc, s, :], x1T[:, cc, ds(c * CH, CH)],
                                     start=(cc == 0), stop=(cc == KC - 1))
                last.then_inc(fp_ready, 1)

            queries_keys(0, ())
            with pe.Fori(0, FH) as h:
                with pe.Fori(0, 2) as qp:
                    scores(PA, None, h, qp)

            def step(b, phase):
                with pe.Fori(0, NCH) as c:
                    pe.wait_ge(tile_read, filled_before(b) + CREDIT)
                    pe.wait_ge(n_ready, b * 2 * NCH * TPC)
                    k = b * 2 * NCH + c
                    transpose_x(k + NCH)
                    pe.wait_ge(v_read, b * NCH + c)
                    project_rows(v_ready, w_inT[:, :, 2 * D:3 * D], 2)
                    pe.wait_ge(o1_ready, b * NCH + c + 1)
                    transpose_rows(o1_tr, 4)
                    pe.wait_ge(o1T_ready, k + 1)
                    pe.wait_ge(y_ready, k)
                    project_rows(yp_ready, w_outT, 6)
                with pe.Fori(0, NCH) as c:
                    pe.wait_ge(n_ready, (b * 2 * NCH + c + 1) * TPC)
                    pe.wait_ge(x1T_ready, b * NCH + c)
                    transpose_rows(x1_tr, 0)
                pe.wait_ge(rt, b * ROUTE_STEPS + 1)
                for cc in range(KC):
                    last = pe.matmul(ps[0:1, 2, 0:NR], xsum[:, cc:cc + 1], wr_sb[:, cc, :],
                                     start=(cc == 0), stop=(cc == KC - 1))
                last.then_inc(rt_mm, 1)
                if phase is PAF:
                    queries_keys(b + 1, ((x1T_ready, (b + 1) * NCH), (rt, b * ROUTE_STEPS + 2)))
                pe.wait_ge(wv_in, (b + 1) * 2 * FH * 16)
                if phase is PAF:
                    pe.wait_ge(q32_ready, (b + 2) * NCH)
                    pe.wait_ge(k32_ready, (b + 2) * NCH * 2)
                for c in range(NCH):
                    if c >= 2:
                        pe.wait_ge(fv_read, b * NCH + c - 1)
                    project_rows(fv_ready, wv_sel, 2 + 2 * (c % 2), x1T[:, :, c * CH:(c + 1) * CH])

                with pe.Fori(0, NCH) as c:
                    for s in range(2):
                        project_chunk(b, 0, c, s)
                with pe.Fori(0, FH) as h:
                    with pe.Fori(0, 2) as qp:
                        scores(phase, b, h, qp)

                with pe.Fori(0, NCH) as c:
                    pe.wait_ge(tile_read, filled_before(b) + CREDIT + BODIES * phase.tiles)
                    k = (b * 2 + 1) * NCH + c
                    pe.wait_ge(fo_stage, b * NCH + c + 1)
                    transpose_rows(o1_tr, 4)
                    pe.wait_ge(o1T_ready, k + 1)
                    pe.wait_ge(y_ready, k)
                    project_rows(yp_ready, wo_sb, 6)

            next_batches(pe, step)

        @block.scalar
        def _(act):
            act.wait_ge(const_made, 4)
            act.activation(frec[0:1, :], one[:, :], ACT.Copy).then_inc(tile_read, CREDIT)
            def chunk_copy(done, src_bank):
                act.activation(chunkT, ps[:, src_bank:src_bank + 2, :], ACT.Copy).then_inc(done, 1)

            def keys(b, free):
                with act.Fori(0, NCH) as c:
                    k = b * NCH + c
                    act.wait_ge(wT_read, 3)
                    for what, count in free:
                        act.wait_ge(what, count)
                    act.wait_ge(x_tr, (b * 2 * NCH + c + 1) * TPC)
                    act.wait_ge(qk_ready, k * 4)
                    chunk_copy(xT_ready, 0)
                    act.wait_ge(k_split, k * K_STEPS)
                    for s in (2, 3):
                        act.wait_ge(qk_ready, k * 4 + s + 1)
                        act.activation(qk32[:, s, :], bank(2 + s), ACT.Identity,
                                       bias=qk_bias[:, s:s + 1]).then_inc(k32_ready, 1)

            def exps(phase, b, h, qp):
                it = h * 2 + qp
                start = filled_before(b) + it * phase.tiles
                mins = mins_before(b) + it * len(phase.mins)
                for tile in phase.act:
                    kind, u, n = tile
                    par, jj = u // UNITS, u % UNITS
                    src = ring(phase.slot[tile])
                    if kind == "A":
                        act.wait_ge(min_ready, mins + phase.min_no[tile])
                        where = (slice(None), n % HALF, TPC * jj + n // HALF, ds(it * 2 + par, 1))
                        act.activation(src, src, ACT.Exp, bias=nmax[where], scale=-1.0,
                                       accum_out=esum[where]).then_inc(tile_read, 1)
                    elif kind == "F":
                        if n == 0:
                            act.wait_ge(min_ready, mins + phase.min_no["F", u, 1])
                        act.activation(probs[:, n * TILE:(n + 1) * TILE], src, ACT.Exp,
                                       bias=fnmax[:, :], scale=-1.0).then_inc(tile_read, 1)
                    else:
                        act.wait_ge(filled, start + phase.fill_no[tile])
                        act.wait_ge(pv_done, (b * FH * NT + it * N_BODY + u) * 2)
                        act.activation(probsT[:, n, :], src, ACT.Copy).then_inc(tile_read, 1)

            keys(0, ())
            with act.Fori(0, FH) as h:
                with act.Fori(0, 2) as qp:
                    exps(PA, None, h, qp)

            def step(b, phase):
                act.wait_ge(comb, b * COMB_STEPS + 2)
                act.activation(stats32[:, 1:3, :], stats32[:, 1:3, :], ACT.Exp).then_inc(comb_e, 1)

                def roots(n):
                    act.wait_ge(ln, n * LN_STEPS + 1)
                    act.activation(rstd[:, :], var[:, :], ACT.Sqrt).then_inc(ln_sq, 1)

                with act.Fori(0, NCH) as c:
                    k = b * 2 * NCH + c
                    act.wait_ge(x_tr, (k + NCH + 1) * TPC)
                    act.wait_ge(yp_ready, k)
                    chunk_copy(xT_ready, 0)
                    act.wait_ge(o1_tr, k + 1)
                    act.wait_ge(v_ready, b * NCH + c + 1)
                    chunk_copy(o1T_ready, 4)
                roots(b * 2)
                with act.Fori(0, NCH) as c:
                    act.wait_ge(x1_tr, b * NCH + c + 1)
                    act.activation(x1T[:, :, ds(c * CH, CH)], ps[:, 0:2, :], ACT.Copy).then_inc(x1T_ready, 1)
                act.wait_ge(rt, b * ROUTE_STEPS + 3)
                act.activation(route[:, NR:2 * NR], route[:, 0:NR], ACT.Exp, bias=route[:, 48:49],
                               accum_out=route[:, 49:50]).then_inc(rt_e, 1)
                if phase is PAF:
                    keys(b + 1, ((yp_ready, (b * 2 + 1) * NCH), (n_ready, (b * 2 + 1) * NCH * TPC)))
                with act.Fori(0, FH) as h:
                    act.wait_ge(n_ready, (b * 2 + 1) * NCH * TPC)
                    if phase is PAF:
                        act.wait_ge(q_split, (b + 2) * NCH * Q_STEPS)
                        act.wait_ge(k_split, (b + 2) * NCH * K_STEPS)
                    with act.Fori(0, 2) as qp:
                        exps(phase, b, h, qp)
                with act.Fori(0, NCH) as c:
                    act.wait_ge(fsp, (b + 1) * PROJ)
                    k = (b * 2 + 1) * NCH + c
                    act.wait_ge(o1_tr, k + 1)
                    act.wait_ge(yp_ready, k)
                    chunk_copy(o1T_ready, 4)
                roots(b * 2 + 1)

            next_batches(act, step)

        @block.vector
        def _(dve):
            v_b_in = b_in_rows[:, :].rearrange("p (h c i) -> p c h i", h=AH, c=3)
            dve.wait_ge(const_in, 16 * N_CONST)
            for c in range(2):
                last = dve.tensor_copy(buf_c[0:1, c * D:(c + 1) * D].rearrange("p (h i) -> p h i", h=AH),
                                       v_b_in[0:1, c, :, :])
            last.then_inc(wT_read, 1)
            dve.wait_ge(wT_ready, 1)
            for cc in range(KC):
                nat = ps[:, 2 * cc:2 * cc + 2, :].rearrange("p a n -> p (a n)")[:, 0:3 * D].rearrange(
                    "p (h c i) -> p c h i", h=AH, c=3)
                for c in range(3):
                    dve.tensor_copy(w_inT[:, cc, c * D:(c + 1) * D].rearrange("p (h i) -> p h i", h=AH),
                                    nat[:, c, :, :])
                last = dve.tensor_copy(w_outT[:, cc, :], ps[:, 4 + cc, 0:D])
            last.then_inc(wT_read, 1)
            dve.wait_ge(wT_ready, 2)
            dve.tensor_copy(qk_bias[:, :], ps[:, 6, 0:4]).then_inc(wT_read, 1)
            dve.wait_ge(wT_read, 3)

            def queries(b, free, used):
                with dve.Fori(0, NCH) as c:
                    k = b * NCH + c
                    level = lambda lv: split[:, 0, :, lv, ds(c * CH, CH)]
                    queries, rest = qk32[:, 0:2, :], rest32[:, 0:2, :]
                    for what, count in free:
                        dve.wait_ge(what, count)
                    dve.wait_ge(filled, used)
                    dve.wait_ge(qk_ready, k * 4 + 2)
                    dve.wait_ge(q_split, k * Q_STEPS)
                    for s in range(2):
                        last = dve.tensor_scalar(qk32[:, s, :], bank(2 + s), qk_bias[:, s:s + 1],
                                                 -float(AD) ** -0.5, ALU.add, ALU.mult)
                    last.then_inc(q32_ready, 1)
                    dve.wait_ge(q32_ready, k + 1)
                    dve.tensor_copy(level(0), queries).then_inc(q_split, 1)
                    dve.wait_ge(q_split, k * Q_STEPS + 1)
                    dve.tensor_tensor(rest, queries, level(0), ALU.subtract).then_inc(q_split, 1)
                    dve.wait_ge(q_split, k * Q_STEPS + 2)
                    dve.tensor_copy(level(1), rest).then_inc(q_split, 1)
                    dve.wait_ge(q_split, k * Q_STEPS + 3)
                    dve.tensor_tensor(level(2), rest, level(1), ALU.subtract).then_inc(q_split, 1)

            def read_chunk(b, hh, c, s):
                k = b * PROJ + hh * NCH + c
                if s == 0:
                    dve.wait_ge(fsp, k)
                dve.wait_ge(fp_ready, k * 2 + s + 1)
                dve.tensor_scalar(f32s[:, s, :], bank(FP_BANK), bqk_sel[:, s:s + 1],
                                  -float(FD) ** -0.5 if s == 0 else 1.0, ALU.add, ALU.mult).then_inc(fp_read, 1)

            def minima(phase, b, h, qp):
                it = h * 2 + qp
                start = filled_before(b) + it * phase.tiles
                units = 0 if b is None else b * FH * NT + it * N_BODY
                for tile in phase.dve:
                    kind, u, n = tile
                    par, jj = u // UNITS, u % UNITS
                    if kind in "AF":
                        dve.wait_ge(filled, start + phase.fill_no[tile])
                        src = ring(phase.slot[tile])
                    if kind == "A":
                        dve.tensor_reduce(nmax[:, n % HALF, TPC * jj + n // HALF, ds(it * 2 + par, 1)],
                                          src, AX.X, ALU.min).then_inc(min_ready, 1)
                    elif kind == "F":
                        last = dve.tensor_reduce(fmin[:, n:n + 1], src, AX.X, ALU.min)
                        if n == 1:
                            last.then_inc(fmin_ready, 1)
                            dve.wait_ge(fmin_ready, units + u + 1)
                            dve.wait_ge(tile_read, start + CREDIT + (
                                phase.read_no["F", u - 1, 1] if u else
                                phase.read_no["F", N_BODY - 1, 1] - phase.tiles))
                            dve.tensor_reduce(fnmax[:, :], fmin[:, :], AX.X, ALU.min).then_inc(min_ready, 1)
                    elif kind == "P":
                        read_chunk(b, h + 1, qp * 2 + par, n)
                    else:
                        dve.wait_ge(pv_done, (units + u + 1) * 2)
                        dve.reciprocal(frec[:, :], ps[:, O_BANK, FD:FD + 1]).then_inc(o_rec, 1)
                        dve.wait_ge(o_rec, units + u + 1)
                        dve.tensor_scalar(fo[:, ds(qp * N_BODY + u, 1), ds(h * FD, FD)],
                                          ps[:, O_BANK, 0:FD], frec[:, :], None, ALU.mult).then_inc(o_read, 1)

            queries(0, (), 0)
            with dve.Fori(0, FH) as h:
                with dve.Fori(0, 2) as qp:
                    minima(PA, None, h, qp)

            def step(b, phase):
                n = NT * AH
                lows = nmax[:, :, :, :].rearrange("p f t a -> p f (t a)")
                sums = esum[:, :, :, :].rearrange("p f t a -> p f (t a)")
                base = b * COMB_STEPS
                dve.wait_ge(tile_read, filled_before(b) + CREDIT)
                dve.wait_ge(k_split, (b + 1) * NCH * K_STEPS)
                dve.tensor_tensor(stats32[:, 0, :], lows[:, 0, :], lows[:, 1, :], ALU.min).then_inc(comb, 1)
                dve.wait_ge(comb, base + 1)
                dve.tensor_tensor(stats32[:, 1:3, :], stats32[:, 0:1, :].to_broadcast([P, HALF, n]), lows,
                                  ALU.subtract).then_inc(comb, 1)
                dve.wait_ge(comb_e, b + 1)
                dve.tensor_tensor(stats32[:, 1:3, :], stats32[:, 1:3, :], sums, ALU.mult).then_inc(comb, 1)
                dve.wait_ge(comb, base + 3)
                dve.tensor_tensor(stats32[:, 3, :], stats32[:, 1, :], stats32[:, 2, :], ALU.add).then_inc(comb, 1)
                dve.wait_ge(comb, base + 4)
                dve.reciprocal(stats32[:, 4, :], stats32[:, 3, :]).then_inc(comb, 1)
                dve.wait_ge(comb, base + 5)
                dve.tensor_tensor(att[:, :, :].rearrange("p t a -> p (t a)"), stats32[:, 3, :], stats32[:, 4, :],
                                  ALU.mult).then_inc(comb, 1)
                dve.drain()

                def add_rows(k, c):
                    dve.wait_ge(yp_ready, k + 1)
                    dve.wait_ge(res_ready, k + 1)
                    for j in range(2):
                        last = dve.tensor_tensor(y[:, ds(c * TPC + 2 * j, 2), :], bank_rows(6 + j),
                                                 rows_in[:, 2 * j:2 * j + 2, :], ALU.add)
                    last.then_inc(y_ready, 1)
                    dve.drain()
                    for t in range(TPC):
                        last = dve.bn_stats(st[:, t, :], flat(y[:, ds(c * TPC + t, 1), :]))
                    last.then_inc(bn_ready, 1)
                    dve.drain()
                    for t in range(TPC):
                        last = dve.bn_aggr(mv_chunk[:, t, :], st[:, t, :])
                    last.then_inc(bn_ready, 1)
                    dve.wait_ge(bn_ready, k * BN_STEPS + 2)
                    dve.tensor_copy(mv[:, ds(c * TPC, TPC), :], mv_chunk[:, :, :]).then_inc(bn_ready, 1)
                    dve.wait_ge(bn_ready, k * BN_STEPS + 3)

                def norm_factors(n):
                    base = n * LN_STEPS
                    dve.tensor_scalar(var[:, :], mv[:, :, 1], EPS, None, ALU.add).then_inc(ln, 1)
                    dve.wait_ge(ln_sq, n + 1)
                    dve.reciprocal(rstd[:, :], rstd[:, :]).then_inc(ln, 1)
                    dve.wait_ge(ln, base + 2)
                    dve.tensor_tensor(newt[:, :], rstd[:, :], rstd[:, :], ALU.mult).then_inc(ln, 1)
                    dve.wait_ge(ln, base + 3)
                    dve.tensor_tensor(newt[:, :], newt[:, :], var[:, :], ALU.mult).then_inc(ln, 1)
                    dve.wait_ge(ln, base + 4)
                    dve.tensor_scalar(newt[:, :], newt[:, :], -0.5, 1.5, ALU.mult, ALU.add).then_inc(ln, 1)
                    dve.wait_ge(ln, base + 5)
                    dve.tensor_tensor(rstd[:, :], rstd[:, :], newt[:, :], ALU.mult).then_inc(ln, 1)
                    dve.drain()

                def norm_chunk(k, c):
                    dve.wait_ge(n_out, k * 16)
                    for t in range(TPC):
                        at = c * TPC + t
                        last = dve.tensor_scalar(rows_mid[:, t, :], flat(y[:, ds(at, 1), :]), mv[:, ds(at, 1), 0],
                                                 rstd[:, ds(at, 1)], ALU.subtract, ALU.mult)
                    last.then_inc(n_ready, TPC)

                with dve.Fori(0, NCH) as c:
                    k = b * 2 * NCH + c
                    dve.wait_ge(v_ready, b * NCH + c + 1)
                    dve.wait_ge(o1_tr, k)
                    dve.wait_ge(n_out, b * 2 * NCH * 16)
                    heads = lambda ap: ap.rearrange("p t (h i) -> p t h i", h=AH)
                    for j in range(2):
                        last = dve.tensor_tensor(heads(rows_mid[:, 2 * j:2 * j + 2, :]), heads(bank_rows(2 + j)),
                                                 v_b_in[:, 2:3, :, :].to_broadcast([P, 2, AH, AD]), ALU.add)
                    last.then_inc(v_read, 1)
                    dve.wait_ge(v_read, b * NCH + c + 1)
                    dve.tensor_tensor(heads(rows_mid), heads(rows_mid),
                                      att[:, ds(c * TPC, TPC), :].unsqueeze(3).to_broadcast([P, TPC, AH, AD]),
                                      ALU.mult).then_inc(o1_ready, 1)
                    add_rows(k, c)
                norm_factors(b * 2)
                with dve.Fori(0, NCH) as c:
                    dve.wait_ge(o1_tr, b * 2 * NCH + NCH)
                    dve.wait_ge(x1_tr, b * NCH + c)
                    norm_chunk(b * 2 * NCH + c, c)

                base = b * ROUTE_STEPS
                logits, probs_r = route[:, 0:NR], route[:, NR:2 * NR]
                best, order, low, total, rec, back = (route[:, 32:40], route[:, 40:48], route[:, 48:49],
                                                      route[:, 49:50], route[:, 50:51], route[:, 52:60])
                dve.wait_ge(x1T_ready, (b + 1) * NCH)
                dve.tensor_reduce(xsum[:, :], x1T[:, :, :], AX.X, ALU.add).then_inc(rt, 1)
                dve.wait_ge(rt_mm, b + 1)
                dve.scalar_tensor_tensor(logits, ps[0:1, 2, 0:NR], 1.0 / L, br_row[:, :],
                                         ALU.mult, ALU.add).then_inc(rt, 1)
                dve.wait_ge(rt, base + 2)
                dve.tensor_reduce(low, logits, AX.X, ALU.max, negate=True).then_inc(rt, 1)
                dve.wait_ge(rt_e, b + 1)
                dve.reciprocal(rec, total).then_inc(rt, 1)
                dve.wait_ge(rt, base + 4)
                dve.tensor_scalar(probs_r, probs_r, rec, None, ALU.mult).then_inc(rt, 1)
                dve.drain()
                dve.max(best, probs_r).then_inc(rt, 1)
                dve.drain()
                dve.max_index(top_i[:, :], best, probs_r).then_inc(rt, 1)
                dve.wait_ge(rt, base + 7)
                dve.tensor_copy(order, top_i[:, :]).then_inc(rt, 1)
                dve.wait_ge(rt, base + 8)
                dve.memset(order[:, FH:8], -float(NR))
                dve.tensor_scalar(order[:, 0:FH], order[:, 0:FH], -1.0, None, ALU.mult).then_inc(rt, 1)
                dve.drain()
                dve.max(back, order).then_inc(rt, 1)
                dve.wait_ge(rt, base + 10)
                dve.tensor_scalar(head_i[:, :], back, -1.0, None, ALU.mult).then_inc(rt, 1)

                if phase is PAF:
                    queries(b + 1, (), filled_before(b))
                with dve.Fori(0, NCH // 2) as pair:
                    for half in range(2):
                        c = pair * 2 + half
                        dve.wait_ge(wv_in, (b + 1) * 2 * FH * 16)
                        dve.wait_ge(fv_ready, b * NCH + c + 1)
                        for t in range(TPC):
                            last = dve.tensor_tensor(
                                vals[:, ds(c * TPC + t, 1), :, 0:FD].rearrange("p a h n -> p (a h) n"),
                                ps[:, 2 + 2 * half + t // 2, (t % 2) * D:(t % 2 + 1) * D].rearrange("p (h n) -> p h n", h=FH),
                                bv_sel[:, :].rearrange("p (h n) -> p h n", h=FH), ALU.add)
                        last.then_inc(fv_read, 1)

                with dve.Fori(0, NCH) as c:
                    dve.wait_ge(n_out, (b * 2 + 1) * NCH * 16)
                    if phase is PAF:
                        dve.wait_ge(x_tr, (b * 2 + 3) * NCH * TPC)
                        dve.wait_ge(qk_ready, (b + 2) * NCH * 4)
                    H = P // 2
                    q_to = lambda i: fq[:, 0, i, ds(c * CH, CH)]
                    k_to = lambda i: fk[:, 0, i, ds(c * CH, CH)]
                    q32, k32, q_rest, k_rest = f32s[:, 0, :], f32s[:, 1, :], frest[:, 0, :], frest[:, 1, :]
                    read_chunk(b, 0, c, 0)
                    dve.drain()
                    dve.tensor_copy(q_to(0), q32)
                    dve.drain()
                    dve.tensor_tensor(q_rest, q32, q_to(0), ALU.subtract)
                    dve.drain()
                    dve.tensor_copy(q_to(1), q_rest)
                    dve.drain()
                    dve.tensor_copy(q_to(2)[0:H], q32[0:H])
                    dve.tensor_tensor(q_to(2)[H:P], q_rest[H:P], q_to(1)[H:P], ALU.subtract)
                    read_chunk(b, 0, c, 1)
                    dve.drain()
                    dve.tensor_copy(k_to(0), k32)
                    dve.drain()
                    dve.tensor_tensor(k_rest, k32, k_to(0), ALU.subtract)
                    dve.drain()
                    dve.tensor_copy(fmid, k_rest)
                    dve.drain()
                    dve.tensor_tensor(k_to(1)[0:H], k_rest[0:H], fmid[0:H, :], ALU.subtract)
                    dve.tensor_copy(k_to(1)[H:P], k32[H:P])
                    dve.tensor_copy(k_to(0)[H:P], fmid[H:P, :]).then_inc(fsp, 1)
                    dve.drain()
                with dve.Fori(0, FH) as h:
                    with dve.Fori(0, 2) as qp:
                        minima(phase, b, h, qp)

                with dve.Fori(0, NCH) as c:
                    add_rows((b * 2 + 1) * NCH + c, c)
                norm_factors(b * 2 + 1)
                with dve.Fori(0, NCH) as c:
                    dve.wait_ge(o1_tr, (b + 1) * 2 * NCH)
                    norm_chunk((b * 2 + 1) * NCH + c, c)

            next_batches(dve, step)


_INS = ["x", "w_in", "b_in", "w_out", "b_out"]
_ALL = ["L0_attn_" + n for n in _INS] + ["L0_ffn_" + n for n in
                                         ("Wq", "bq", "Wk", "bk", "Wv", "bv", "Wr", "br", "Wo", "bo")]


def kernel(**inputs):
    import numpy as _np
    import concourse.bacc as _bacc
    from concourse import mybir as _mybir
    from concourse.bass_utils import run_bass_kernel_spmd as _run

    nc = _bacc.Bacc("TRN2", target_bir_lowering=False, num_devices=1)
    arrays, args = {}, []
    for name in _ALL:
        a = _np.ascontiguousarray(inputs[name])
        arrays[f"in_{name}"] = a
        args.append(nc.dram_tensor(f"in_{name}", a.shape, _mybir.dt.from_np(a.dtype), kind="ExternalInput").ap())
    out = nc.dram_tensor("out_rows", (B, L, D), _mybir.dt.float32, kind="ExternalOutput").ap()
    build(nc, *args, out)
    r = _run(nc, [arrays], core_ids=[0])
    return r.results[0]["out_rows"]
```

```python
import concourse.bass as bass
from concourse import mybir
from contextlib import ExitStack

F32 = mybir.dt.float32
BF16 = mybir.dt.bfloat16
U32 = mybir.dt.uint32
I32 = mybir.dt.int32
ALU = mybir.AluOpType
ACT = mybir.ActivationFunctionType
AX = mybir.AxisListType
ds = bass.ds

P = 128
B, L, D = 4, 2048, 256
NT = L // P
KC = D // P
CH = 512
NCH = L // CH
TPC = CH // P
AH, AD = 16, D // 16
GH = P // AD
FH, FD = 4, 64
NR = 16
LV = 3
Q_LEVEL = (0, 0, 0, 1, 1, 2)
K_LEVEL = (0, 1, 2, 0, 1, 0)
SK = len(Q_LEVEL) * AD
TILE = 1024
HALF = L // TILE
EPS = 1e-5
SLOTS = 3
A_SLOTS = 4
UNITS = 4
CREDIT = A_SLOTS


def schedule(mode):
    pe, act, dve = [], [], []
    units = range(2 * UNITS)
    if mode == "A":
        pe = [("A", u, i) for u in units for i in range(8)]
        return pe, pe, pe
    if mode == "AF":
        for u in units:
            A = lambda *i: [("A", u, n) for n in i]
            Q = lambda i: [("Q", u, i)]
            F = [("F", u, 0), ("F", u, 1)]
            proj = [("P", u, u % UNITS)] * (u % UNITS < 2)
            pe += A(0) + proj + F + A(1) + Q(0) + A(2, 3) + Q(1) + A(4) + Q(2) + [("PV", u, 0)] + A(5) \
                + Q(3) + A(6, 7) + [("PV", u, 1)]
            act += A(0) + F + Q(0) + A(1) + Q(1) + A(2, 3) + Q(2) + A(4) + Q(3) + A(5) + [("W", u, 0)] + A(6, 7)
            dve += A(0) + proj + F + A(1, 2, 3, 4, 5, 6, 7) + [("O", u, 0)]
        return pe, act, dve
    F = lambda u, n: [("F", u, n)] * (u < 2 * UNITS)
    W = lambda u: [("W", u, 0)] * (u < 2 * UNITS)
    proj = lambda u, n: [("P", u, n)] * (u % UNITS == 0)
    pe += F(0, 0) + F(0, 1)
    act += F(0, 0) + F(0, 1) + W(0)
    dve += F(0, 0) + F(0, 1)
    for u in units:
        pe += F(u + 1, 0) + [("T", u, 0)] + proj(u, 0) + F(u + 1, 1) + [("T", u, 1)] + proj(u, 1) \
            + [("PV", u, 0), ("PV", u, 1)]
        act += [("T", u, 0)] + F(u + 1, 0) + [("T", u, 1)] + F(u + 1, 1) + W(u + 1)
        dve += F(u + 1, 0) + proj(u, 0) + F(u + 1, 1) + proj(u, 1) + [("O", u, 0)]
    return pe, act, dve


def slots_of(mode, fills):
    slots, n = {}, 0
    for tile in fills:
        if tile[0] == "Q":
            slots[tile] = "own"
        elif mode == "F":
            slots[tile] = {"F": tile[2], "T": 2}[tile[0]]
        else:
            slots[tile] = n % (A_SLOTS if mode == "A" else SLOTS)
            n += 1
    return slots


def build(nc, x, w_in, b_in, w_out, b_out, wq, bq, wk, bk, wv, bv, wr, br, wo, bo, out):
    ctx = ExitStack()
    with ctx:
        sb = lambda name, shape, dt=F32: ctx.enter_context(nc.sbuf_tensor(name, shape, dt))
        sem = lambda name: ctx.enter_context(nc.semaphore(name))
        ctx.enter_context(nc.allow_non_contiguous_dma(reason="bias columns"))

        x1_dram = nc.dram_tensor("x1_rows", [NT, P, D], F32).ap()
        ident = sb("ident", [P, P])
        w_inT = sb("w_inT", [P, KC, 3 * D])
        w_outT = sb("w_outT", [P, KC, D])
        wo_sb = sb("wo_sb", [P, KC, D])
        wr_sb = sb("wr_sb", [P, KC, NR])
        b_in_rows = sb("b_in_rows", [P, 3 * D])
        b_out_rows = sb("b_out_rows", [P, D])
        bo_rows = sb("bo_rows", [P, D])
        br_row = sb("br_row", [1, NR])
        qk_bias = sb("qk_bias", [P, 4])
        wv_sel = sb("wv_sel", [P, KC, FH * FD])
        bv_sel = sb("bv_sel", [P, FH * FD])
        wqk_sel = sb("wqk_sel", [P, KC, 2, 2 * FD])
        bqk_sel = sb("bqk_sel", [P, 2])
        one = sb("one", [1, 1])

        split = sb("split", [P, 2, 2, LV, L], BF16)
        stack = sb("stack", [P, 2, 2, L], BF16)
        fq_mem = sb("fq_mem", [P, 3 * L])
        fq = fq_mem[:, :].bitcast(BF16).rearrange("p (a s l) -> p a s l", a=2, s=3)
        fk_mem = sb("fk_mem", [P, 2 * L])
        fk = fk_mem[:, :].bitcast(BF16).rearrange("p (a s l) -> p a s l", a=2, s=2)
        rows_q = fq_mem[:, 0:NT * D].rearrange("p (t d) -> p t d", t=NT)
        rows_k = fk_mem[:, :].rearrange("p (t d) -> p t d", t=NT)
        stats32 = fq_mem[:, NT * D:NT * D + 6 * NT * AH].rearrange("p (s n) -> p s n", s=6)
        vals = sb("vals", [P, NT, FH, FD + 1])
        x1T = sb("x1T", [P, KC, L])
        fo = sb("fo", [P, NT, FH * FD])
        shared = sb("shared", [P, 2 * L])
        probs = shared[:, 0:L]
        probsT = shared[:, L:2 * L].rearrange("p (f k) -> p f k", f=HALF)
        y = shared[:, :].rearrange("p (t d) -> p t d", t=NT)
        qk32 = shared[:, 0:L].rearrange("p (s n) -> p s n", s=4)
        rest32 = shared[:, L:2 * L].rearrange("p (s n) -> p s n", s=4)
        w_rows = shared[:, 0:6 * D].rearrange("p (t d) -> p t d", t=6)
        w_out_rows = shared[:, 6 * D:8 * D].rearrange("p (t d) -> p t d", t=KC)
        buf_a = sb("buf_a", [P, TPC * D])
        buf_b = sb("buf_b", [P, TPC * D])
        buf_c = sb("buf_c", [P, TPC * D])
        xT = [b[:, :].rearrange("p (c n) -> p c n", c=KC) for b in (buf_a, buf_b)]
        oT = buf_c[:, :].rearrange("p (c n) -> p c n", c=KC)
        f32s = buf_a[:, :].rearrange("p (s n) -> p s n", s=2)
        frest = buf_b[:, :].rearrange("p (s n) -> p s n", s=2)
        fmid = buf_c[:, 0:CH // 2].bitcast(BF16)

        nmax = sb("nmax", [P, HALF, NT, AH])
        esum = sb("esum", [P, HALF, NT, AH])
        att = sb("att", [P, NT, AH])
        fmin = sb("fmin", [P, 2, HALF])
        fnmax = sb("fnmax", [P, 2])
        fweight = sb("fweight", [P, 2, HALF])
        fsum = sb("fsum", [P, FD + 1])
        frec = sb("frec", [P, 1])
        mv = sb("mv", [P, NT, 2])
        st = sb("st", [P, TPC, 6])
        mv_chunk = sb("mv_chunk", [P, TPC, 2])
        var = sb("var", [P, NT])
        rstd = sb("rstd", [P, NT])
        newt = sb("newt", [P, NT])
        xsum = sb("xsum", [P, KC])
        xsums = sb("xsums", [P, KC, NCH])
        route = sb("route", [1, 4 * NR])
        top_i = sb("top_i", [1, 8], U32)
        head_i = sb("head_i", [1, 8], I32)

        ps = ctx.enter_context(nc.psum_tensor("ps", [P, 8, CH], F32))
        O_BANK, FP_BANK = 6, 7
        bank = lambda n: ps[:, n, :]
        bank_rows = lambda n: ps[:, n, :].rearrange("p (t d) -> p t d", d=D)

        const_in = sem("const_in")
        const_made = sem("const_made")
        wT_ready = sem("wT_ready")
        wT_read = sem("wT_read")
        x_in = sem("x_in")
        mid_in = sem("mid_in")
        x_tr = sem("x_tr")
        xT_ready = sem("xT_ready")
        qk_ready = sem("qk_ready")
        q32_ready = sem("q32_ready")
        k32_ready = sem("k32_ready")
        q_split = sem("q_split")
        k_split = sem("k_split")
        stack_in = [sem("stack_in_even"), sem("stack_in_odd")]
        filled = sem("filled")
        min_ready = sem("min_ready")
        low_ready = sem("low_ready")
        w_ready = sem("w_ready")
        tile_read = sem("tile_read")
        pv_done = sem("pv_done")
        o_read = sem("o_read")
        comb = sem("comb")
        comb_e = sem("comb_e")
        v_ready = sem("v_ready")
        v_read = sem("v_read")
        o1_ready = sem("o1_ready")
        o1_tr = sem("o1_tr")
        o1T_ready = sem("o1T_ready")
        res_in = sem("res_in")
        res_ready = sem("res_ready")
        yp_ready = sem("yp_ready")
        y_ready = sem("y_ready")
        bn_ready = sem("bn_ready")
        ln = sem("ln")
        ln_sq = sem("ln_sq")
        n_ready = sem("n_ready")
        n_out = sem("n_out")
        x1_tr = sem("x1_tr")
        x1T_ready = sem("x1T_ready")
        rt = sem("rt")
        rt_mm = sem("rt_mm")
        rt_e = sem("rt_e")
        wv_in = sem("wv_in")
        fv_ready = sem("fv_ready")
        fv_read = sem("fv_read")
        fpw_in = sem("fpw_in")
        fp_ready = sem("fp_ready")
        fp_read = sem("fp_read")
        split_act = sem("split_act")
        split_dve = sem("split_dve")
        fsp = sem("fsp")

        N_BODY = 2 * UNITS
        BODIES = FH * 2
        Q_STEPS = K_STEPS = 4
        LN_STEPS, BN_STEPS = 6, 3
        COMB_STEPS = 6
        ROUTE_STEPS = 11
        N_CONST = 8
        HEAD_DMAS = 12
        SEL_DMAS = 8
        SPLIT_ACT, SPLIT_DVE = 4, 2
        PROJ = (FH + 1) * NCH

        class Phase:
            def __init__(self, mode):
                self.mode = mode
                self.pe, self.act, self.dve = schedule(mode)
                self.fills = [t for t in self.pe if t[0] in "AFTQ"]
                self.reads = [t for t in self.act if t[0] in "AFTQ"]
                self.tiles = len(self.fills)
                self.mins = [t for t in self.dve if t[0] in "AF"]
                self.slot = slots_of(mode, self.fills)
                self.fill_no = {t: n + 1 for n, t in enumerate(self.fills)}
                self.read_no = {t: n + 1 for n, t in enumerate(self.reads)}
                self.min_no = {t: n + 1 for n, t in enumerate(self.mins)}

            def before(self, tile):
                n = self.fill_no[tile] - 1
                for j in range(n - 1, -1, -1):
                    if self.slot[self.fills[j]] == self.slot[tile]:
                        return self.read_no[self.fills[j]]
                return max(self.read_no[t] for t in self.fills if self.slot[t] == self.slot[tile]) - self.tiles

        PA, PAF, PF = Phase("A"), Phase("AF"), Phase("F")

        def filled_before(b):
            return 0 if b is None else BODIES * (PA.tiles + PAF.tiles * b)

        def mins_before(b):
            return 0 if b is None else BODIES * (len(PA.mins) + len(PAF.mins) * b)

        H = P // 2
        q32, k32, q_rest, k_rest = f32s[:, 0, :], f32s[:, 1, :], frest[:, 0, :], frest[:, 1, :]

        def q_to(i, c, par=0):
            return fq[:, par, i, ds(c * CH, CH)]

        def k_to(i, c, par=0):
            return fk[:, par, i, ds(c * CH, CH)]

        def flat(ap):
            return ap.rearrange("p a n -> p (a n)")

        def ring(slot):
            return flat(ps[:, 2 * slot:2 * slot + 2, :])

        def next_batches(eng, step):
            with eng.Fori(0, B - 1) as b:
                step(b, PAF)
            step(B - 1, PF)

        block = ctx.enter_context(nc.Block())

        @block.sync
        def _(sp):
            row = lambda v: v.rearrange("(a n) -> a n", a=1)
            sp.dma_start(w_rows, w_in.rearrange("(t p) d -> p t d", p=P)).then_inc(const_in, 16)
            sp.dma_start(w_out_rows, w_out.rearrange("(t p) d -> p t d", p=P)).then_inc(const_in, 16)
            sp.dma_start(wo_sb[:, :, :], wo.rearrange("(c p) n -> p c n", p=P)).then_inc(const_in, 16)
            sp.dma_start(wr_sb[:, :, :], wr.rearrange("(c p) n -> p c n", p=P)).then_inc(const_in, 16)
            sp.dma_start(b_in_rows[:, :], b_in.partition_broadcast(P)).then_inc(const_in, 16)
            sp.dma_start(b_out_rows[:, :], b_out.partition_broadcast(P)).then_inc(const_in, 16)
            sp.dma_start(bo_rows[:, :], bo.partition_broadcast(P)).then_inc(const_in, 16)
            sp.dma_start(br_row[:, :], row(br)).then_inc(const_in, 16)

            x_rows = x.rearrange("b (t p) d -> (b t) p d", p=P)
            out_tiles = out.rearrange("b (t p) d -> (b t) p d", p=P)

            def load_rows(dst, src, done, free):
                with sp.Fori(0, NCH) as c:
                    for what, count in free:
                        sp.wait_ge(what, count)
                    sp.dma_start(dst[:, ds(c * TPC, TPC), :], src(c).rearrange("t p d -> p t d")).then_inc(done, 16)

            x_chunk = lambda b: lambda c: x_rows[ds((b * NCH + c) * TPC, TPC), :, :]

            def stack_heads(b, before, tiles, load_head=None):
                with sp.Fori(0, 2) as hh:
                    sp.wait_ge(q_split, (b + 1) * NCH * Q_STEPS)
                    sp.wait_ge(k_split, (b + 1) * NCH * K_STEPS)
                    for r in range(GH):
                        sp.wait_ge(filled, before + (hh * (GH - 1) * tiles if r == 0 else (hh * GH + r - 1) * tiles))
                        for side, levels in ((0, Q_LEVEL), (1, K_LEVEL)):
                            for g, lv in enumerate(levels):
                                sp.dma_start(stack[g * AD:(g + 1) * AD, r % 2, side, :],
                                             flat(split[r * AD:(r + 1) * AD, side, ds(hh, 1), lv, :])
                                             ).then_inc(stack_in[r % 2], 16)
                        if load_head and r % UNITS == 0:
                            load_head(hh * 2 + r // UNITS + 1)

            load_rows(rows_k, x_chunk(0), x_in, ())
            load_rows(rows_q, x_chunk(0), mid_in, ())
            stack_heads(0, 0, PA.tiles // 2)

            def step(b, phase):
                if phase is PAF:
                    load_rows(rows_k, x_chunk(b + 1), x_in,
                              ((y_ready, b * 2 * NCH), (x_tr, (b * 2 + 1) * NCH)))
                with sp.Fori(0, NCH) as c:
                    sp.wait_ge(n_ready, (b * 2 * NCH + c + 1) * TPC)
                    sp.dma_start(x1_dram[ds(c * TPC, TPC), :, :].rearrange("t p d -> p t d"),
                                 y[:, ds(c * TPC, TPC), :]).then_inc(n_out, 16)
                with sp.Fori(0, FH) as h:
                    sp.wait_ge(rt, (b + 1) * ROUTE_STEPS)
                    i = sp.value_load(head_i[0:1, ds(h % FH, 1)], min_val=0, max_val=NR - 1)
                    sp.dma_start(wv_sel[:, :, ds(h * FD, FD)],
                                 wv[:, ds(i * FD, FD)].rearrange("(c p) n -> p c n", p=P)).then_inc(wv_in, 16)
                    sp.dma_start(bv_sel[:, ds(h * FD, FD)],
                                 bv[ds(i * FD, FD)].partition_broadcast(P)).then_inc(wv_in, 16)

                def load_head(hh):
                    done = (b * PROJ + hh * NCH) * 2
                    i = sp.value_load(head_i[0:1, ds(hh % FH, 1)], min_val=0, max_val=NR - 1)
                    sp.wait_ge(fp_ready, done)
                    sp.wait_ge(fp_read, done)
                    for s, (w, bias) in enumerate(((wq, bq), (wk, bk))):
                        for twice in range(2):
                            sp.dma_start(wqk_sel[:, :, s, twice * FD:(twice + 1) * FD],
                                         w[:, ds(i * FD, FD)].rearrange("(c p) n -> p c n", p=P)).then_inc(fpw_in, 16)
                            sp.dma_start(bqk_sel[twice * FD:(twice + 1) * FD, s:s + 1],
                                         bias[ds(i * FD, FD)].rearrange("(p a) -> p a", a=1)).then_inc(fpw_in, 16)

                with sp.Fori(0, 1 if phase is PAF else FH + 1) as hh:
                    load_head(hh)
                if phase is PAF:
                    stack_heads(b + 1, filled_before(b), PAF.tiles // 2, load_head)

                scored = filled_before(b) + BODIES * phase.tiles
                load_rows(rows_k, lambda c: x1_dram[ds(c * TPC, TPC), :, :], res_in,
                          ((filled, scored), (fsp, (b + 1) * PROJ), (n_out, (b * 2 + 1) * NCH * 16)))
                if phase is PAF:
                    load_rows(rows_q, x_chunk(b + 1), mid_in, ((filled, scored),))
                with sp.Fori(0, NCH) as c:
                    sp.wait_ge(n_ready, ((b * 2 + 1) * NCH + c + 1) * TPC)
                    sp.dma_start(out_tiles[ds((b * NCH + c) * TPC, TPC), :, :].rearrange("t p d -> p t d"),
                                 y[:, ds(c * TPC, TPC), :]).then_inc(n_out, 16)
            next_batches(sp, step)
            sp.wait_ge(n_out, B * 2 * NCH * 16)

        @block.gpsimd
        def _(pool):
            pool.memset(ident[:, :], 0.0).then_inc(const_made, 1)
            pool.memset(one[:, :], 1.0).then_inc(const_made, 1)
            pool.memset(vals[:, :, :, FD:FD + 1], 1.0).then_inc(const_made, 1)
            pool.wait_ge(const_made, 3)
            pool.affine_select(out=ident[:, :], in_=ident[:, :], compare_op=ALU.not_equal, fill=1.0, base=0,
                               pattern=[[-1, P]], channel_multiplier=1).then_inc(const_made, 1)
            def split_keys(b):
                with pool.Fori(0, NCH) as c:
                    k = b * NCH + c
                    level = lambda lv: split[:, 1, :, lv, ds(c * CH, CH)]
                    keys, rest = qk32[:, 2:4, :], rest32[:, 2:4, :]
                    pool.wait_ge(k_split, k * K_STEPS + 1)
                    pool.tensor_tensor(rest, keys, level(0), ALU.subtract).then_inc(k_split, 1)
                    pool.wait_ge(k_split, k * K_STEPS + 3)
                    pool.tensor_tensor(level(2), rest, level(1), ALU.subtract).then_inc(k_split, 1)

            split_keys(0)

            def step(b, phase):
                with pool.Fori(0, NCH) as c:
                    pool.wait_ge(x_tr, (b * 2 + 1) * NCH + c + 1)
                    rows = rows_q[:, ds(c * TPC, TPC), :]
                    pool.tensor_tensor(rows, rows, b_out_rows[:, :].unsqueeze(1).to_broadcast([P, TPC, D]),
                                       ALU.add).then_inc(res_ready, 1)
                if phase is PAF:
                    split_keys(b + 1)
                def split_head(hh, par):
                    with pool.Fori(0, NCH) as c:
                        k = b * PROJ + hh * NCH + c
                        H = P // 2
                        low, high, every = (0, H), (H, P), (0, P)
                        q_to = lambda i, r: flat(fq[r[0]:r[1], ds(par, 1), i, ds(c * CH, CH)])
                        k_to = lambda i, r: flat(fk[r[0]:r[1], ds(par, 1), i, ds(c * CH, CH)])
                        q32, k32 = (lambda r: f32s[r[0]:r[1], 0, :]), (lambda r: f32s[r[0]:r[1], 1, :])
                        qr, kr = (lambda r: frest[r[0]:r[1], 0, :]), (lambda r: frest[r[0]:r[1], 1, :])
                        pool.wait_ge(fp_read, k * 2 + 2)
                        pool.wait_ge(filled, filled_before(b) + (hh - 1) * 2 * phase.tiles)
                        pool.tensor_copy(q_to(0, every), q32(every))
                        pool.drain()
                        pool.tensor_tensor(qr(every), q32(every), q_to(0, every), ALU.subtract)
                        pool.drain()
                        pool.tensor_copy(q_to(1, every), qr(every))
                        pool.drain()
                        pool.tensor_copy(q_to(2, low), q32(low))
                        pool.tensor_copy(k_to(0, low), k32(low))
                        pool.drain()
                        pool.tensor_tensor(kr(low), k32(low), k_to(0, low), ALU.subtract)
                        pool.drain()
                        pool.tensor_copy(fmid[0:H, :], kr(low))
                        pool.drain()
                        pool.tensor_tensor(k_to(1, low), kr(low), fmid[0:H, :], ALU.subtract)
                        pool.drain()
                        pool.tensor_copy(k_to(1, high), k32(high))
                        pool.tensor_tensor(q_to(2, high), qr(high), q_to(1, high), ALU.subtract)
                        pool.drain()
                        pool.tensor_tensor(kr(high), k32(high), k_to(1, high), ALU.subtract)
                        pool.drain()
                        pool.tensor_copy(k_to(0, high), kr(high)).then_inc(fsp, 1)
                        pool.drain()
                with pool.Fori(0, FH) as h:
                    split_head(h + 1, (h + 1) % 2)
                with pool.Fori(0, NCH) as c:
                    pool.wait_ge(res_in, (b + 1) * NCH * 16)
                    rows = rows_k[:, ds(c * TPC, TPC), :]
                    pool.tensor_tensor(rows, rows, bo_rows[:, :].unsqueeze(1).to_broadcast([P, TPC, D]),
                                       ALU.add).then_inc(res_ready, 1)

            next_batches(pool, step)

        @block.tensor
        def _(pe):
            pe.wait_ge(const_made, 4)
            pe.wait_ge(const_in, 16 * N_CONST)
            for cc in range(KC):
                for t in range(6):
                    col = cc * 2 * CH + t * P
                    pe.transpose(ps[:, col // CH, col % CH:col % CH + P],
                                 w_rows[:, t, cc * P:(cc + 1) * P], ident[:, :])
                for t in range(KC):
                    last = pe.transpose(ps[:, 4 + cc, t * P:(t + 1) * P],
                                        w_out_rows[:, t, cc * P:(cc + 1) * P], ident[:, :])
            last.then_inc(wT_ready, 1)
            pe.wait_ge(wT_read, 1)
            for s in range(4):
                last = pe.matmul(ps[:, 6, s:s + 1], buf_c[0:1, s * P:(s + 1) * P], one[:, :],
                                 start=True, stop=True)
            last.then_inc(wT_ready, 1)
            pe.wait_ge(wT_read, 2)

            def project_rows(done, rowsT, w, bank0):
                for t in range(TPC):
                    for cc in range(KC):
                        last = pe.matmul(ps[:, bank0 + t // 2, (t % 2) * D:(t % 2 + 1) * D],
                                         rowsT[:, cc, t * P:(t + 1) * P], w[:, cc, :],
                                         start=(cc == 0), stop=(cc == KC - 1))
                last.then_inc(done, 1)

            def transpose_chunk(done, rows, c, bank0):
                for cc in range(KC):
                    for t in range(TPC):
                        last = pe.transpose(ps[:, bank0 + cc, t * P:(t + 1) * P],
                                            rows[:, c * TPC + t, cc * P:(cc + 1) * P], ident[:, :])
                last.then_inc(done, 1)

            def queries_keys(b, free, router=None):
                def transpose_x(c):
                    pe.wait_ge(xT_ready, b * 2 * NCH + c)
                    transpose_chunk(x_tr, rows_k, c, 0)

                pe.wait_ge(x_in, (b + 1) * NCH * 16)
                for what, count in free:
                    pe.wait_ge(what, count)
                transpose_x(0)
                transpose_x(1)
                if router:
                    router()
                for c in range(NCH):
                    k = b * NCH + c
                    pe.wait_ge(xT_ready, b * 2 * NCH + c + 1)
                    pe.wait_ge(q32_ready, k)
                    pe.wait_ge(k32_ready, k * 2)
                    for s in range(4):
                        for cc in range(KC):
                            last = pe.matmul(bank(2 + s), w_inT[:, cc, s * P:(s + 1) * P], xT[c % 2][:, cc, :],
                                             start=(cc == 0), stop=(cc == KC - 1))
                        last.then_inc(qk_ready, 1)
                    if c + 2 < NCH:
                        transpose_x(c + 2)

            def scores(phase, b, h, qp):
                it = h * 2 + qp
                ab = 0 if b is None else b + 1
                start = filled_before(b) + CREDIT + it * phase.tiles
                if phase is not PF:
                    pe.wait_ge(q32_ready, (ab + 1) * NCH)
                    pe.wait_ge(k32_ready, (ab + 1) * NCH * 2)
                if phase is not PA:
                    pe.wait_ge(fv_read, (b + 1) * NCH)
                    pe.wait_ge(fsp, b * PROJ + (h + 1) * NCH)
                if phase is not PA:
                    projected = (b * PROJ + (h + 1) * NCH + qp * 2) * 2
                for tile in phase.pe:
                    kind, u, n = tile
                    par, jj = u // UNITS, u % UNITS
                    if kind == "PV":
                        last_part = ("Q", u, 2 * n + 1) if phase is PAF else ("T", u, n)
                        pe.wait_ge(tile_read, start + phase.read_no[last_part])
                        if n == 0:
                            pe.wait_ge(o_read, b * FH * NT + it * N_BODY + u)
                        for kt in range(NT // 2):
                            last = pe.matmul(
                                ps[:, O_BANK, n * (FD + 1):(n + 1) * (FD + 1)], probsT[:, n, kt * P:(kt + 1) * P],
                                flat(vals[:, n * (NT // 2) + kt, ds(h, 1), :]),
                                start=(kt == 0), stop=(kt == NT // 2 - 1))
                        last.then_inc(pv_done, 1)
                        continue
                    if kind == "P":
                        project_chunk(b, h + 1, qp * 2 + par, n, projected + par * 2)
                        continue
                    if kind == "Q":
                        before = phase.read_no[("Q", u, n - 1) if n else ("F", u, 0)]
                        pe.wait_ge(tile_read, start + before)
                        for kt in range(TPC):
                            col = n * CH + kt * P
                            last = pe.transpose(ps[:, FP_BANK, kt * P:(kt + 1) * P], probs[:, col:col + P], ident[:, :])
                        last.then_inc(filled, 1)
                        continue
                    slot = phase.slot[tile]
                    pe.wait_ge(tile_read, start + phase.before(tile))
                    if kind == "T":
                        pe.wait_ge(tile_read, start + phase.read_no["F", u, n])
                    if kind == "A" and n == jj == 0:
                        pe.wait_ge(stack_in[par], (ab * BODIES + it + 1) * HEAD_DMAS * 16)
                    for j in range(2):
                        dst = 2 * slot + j
                        if kind == "A":
                            t, col = TPC * jj + n // HALF, (n % HALF) * TILE + j * CH
                            last = pe.matmul(bank(dst), stack[0:SK, par, 0, t * P:(t + 1) * P],
                                             stack[0:SK, par, 1, col:col + CH], start=True, stop=True)
                        elif kind == "F":
                            col = n * TILE + j * CH
                            for s in range(3):
                                last = pe.matmul(bank(dst), flat(fq[:, ds(h % 2, 1), s, ds(qp * TILE + u * P, P)]),
                                                 flat(fk[:, ds(h % 2, 1), s // 2, col:col + CH]),
                                                 start=(s == 0), stop=(s == 2))
                        else:
                            col = n * TILE + j * CH
                            for kt in range(TPC):
                                last = pe.transpose(ps[:, dst, kt * P:(kt + 1) * P],
                                                    probs[:, col + kt * P:col + (kt + 1) * P], ident[:, :])
                    last.then_inc(filled, 1)

            def project_chunk(b, hh, c, s, projected):
                pe.wait_ge(fpw_in, (b * (FH + 1) + hh + 1) * SEL_DMAS * 16)
                pe.wait_ge(fp_read, projected + s)
                for cc in range(KC):
                    last = pe.matmul(bank(FP_BANK), wqk_sel[:, cc, s, :], x1T[:, cc, ds(c * CH, CH)],
                                     start=(cc == 0), stop=(cc == KC - 1))
                last.then_inc(fp_ready, 1)

            queries_keys(0, ())
            with pe.Fori(0, FH) as h:
                with pe.Fori(0, 2) as qp:
                    scores(PA, None, h, qp)

            def step(b, phase):
                def transpose_x(c):
                    pe.wait_ge(xT_ready, (b * 2 + 1) * NCH + c)
                    transpose_chunk(x_tr, rows_q, c, 0)

                def output(c):
                    pe.wait_ge(o1T_ready, b * 2 * NCH + c + 1)
                    pe.wait_ge(y_ready, b * 2 * NCH + c)
                    project_rows(yp_ready, oT, w_outT, 6)

                pe.wait_ge(mid_in, (b + 1) * NCH * 16)
                pe.wait_ge(tile_read, filled_before(b) + CREDIT)
                transpose_x(0)
                transpose_x(1)
                for c in range(NCH):
                    pe.wait_ge(xT_ready, (b * 2 + 1) * NCH + c + 1)
                    pe.wait_ge(v_read, b * NCH + c)
                    project_rows(v_ready, xT[c % 2], w_inT[:, :, 2 * D:3 * D], 2)
                    if c + 2 < NCH:
                        transpose_x(c + 2)
                    if c:
                        output(c - 1)
                    pe.wait_ge(o1_ready, b * NCH + c + 1)
                    pe.wait_ge(o1T_ready, b * 2 * NCH + c)
                    transpose_chunk(o1_tr, fo, c, 4)
                output(NCH - 1)
                for c in range(NCH):
                    pe.wait_ge(n_ready, (b * 2 * NCH + c + 1) * TPC)
                    if c >= 2:
                        pe.wait_ge(x1T_ready, b * NCH + c - 1)
                    transpose_chunk(x1_tr, y, c, 2 * (c % 2))

                def router():
                    pe.wait_ge(rt, b * ROUTE_STEPS + 1)
                    for cc in range(KC):
                        last = pe.matmul(ps[0:1, 6, 0:NR], xsum[:, cc:cc + 1], wr_sb[:, cc, :],
                                         start=(cc == 0), stop=(cc == KC - 1))
                    last.then_inc(rt_mm, 1)

                if phase is PAF:
                    queries_keys(b + 1, ((x1T_ready, (b + 1) * NCH),), router)
                else:
                    router()
                pe.wait_ge(wv_in, (b + 1) * 2 * FH * 16)
                if phase is PAF:
                    pe.wait_ge(q32_ready, (b + 2) * NCH)
                    pe.wait_ge(k32_ready, (b + 2) * NCH * 2)
                for c in range(NCH):
                    if c >= 2:
                        pe.wait_ge(fv_read, b * NCH + c - 1)
                    project_chunk(b, 0, c, 0, (b * PROJ + c) * 2)
                    project_rows(fv_ready, x1T[:, :, c * CH:(c + 1) * CH], wv_sel, 2 + 2 * (c % 2))
                    project_chunk(b, 0, c, 1, (b * PROJ + c) * 2)
                with pe.Fori(0, FH) as h:
                    with pe.Fori(0, 2) as qp:
                        scores(phase, b, h, qp)

                k = (b * 2 + 1) * NCH

                def transpose_fo(c):
                    if c >= 2:
                        pe.wait_ge(o1T_ready, k + c - 1)
                    transpose_chunk(o1_tr, fo, c, 2 * (c % 2))

                pe.wait_ge(tile_read, filled_before(b) + CREDIT + BODIES * phase.tiles)
                pe.wait_ge(o_read, (b + 1) * FH * NT)
                transpose_fo(0)
                transpose_fo(1)
                for c in range(NCH):
                    pe.wait_ge(o1T_ready, k + c + 1)
                    pe.wait_ge(fp_read, (b + 1) * PROJ * 2)
                    if c >= 2:
                        pe.wait_ge(y_ready, k + c - 1)
                    project_rows(yp_ready, xT[c % 2], wo_sb, 4 + 2 * (c % 2))
                    if c + 2 < NCH:
                        transpose_fo(c + 2)

            next_batches(pe, step)

        @block.scalar
        def _(act):
            act.wait_ge(const_made, 4)
            act.activation(frec[0:1, :], one[:, :], ACT.Copy).then_inc(tile_read, CREDIT)
            def chunk_copy(done, dst, src_bank):
                act.activation(dst, ps[:, src_bank:src_bank + 2, :], ACT.Copy).then_inc(done, 1)

            def keys(b, free, router=None):
                def copy_x(c):
                    act.wait_ge(x_tr, b * 2 * NCH + c + 1)
                    if c >= 2:
                        act.wait_ge(qk_ready, (b * NCH + c - 1) * 4)
                    chunk_copy(xT_ready, xT[c % 2], 0)

                act.wait_ge(wT_read, 3)
                for what, count in free:
                    act.wait_ge(what, count)
                copy_x(0)
                copy_x(1)
                if router:
                    router()
                for c in range(NCH):
                    k = b * NCH + c
                    level = lambda lv: split[:, 1, :, lv, c * CH:(c + 1) * CH]
                    act.wait_ge(k_split, k * K_STEPS)
                    for s in (2, 3):
                        act.wait_ge(qk_ready, k * 4 + s + 1)
                        act.activation(qk32[:, s, :], bank(2 + s), ACT.Identity,
                                       bias=qk_bias[:, s:s + 1]).then_inc(k32_ready, 1)
                    act.wait_ge(k32_ready, k * 2 + 2)
                    act.activation(level(0), qk32[:, 2:4, :], ACT.Copy).then_inc(k_split, 1)
                    if c + 2 < NCH:
                        copy_x(c + 2)
                    act.wait_ge(k_split, k * K_STEPS + 2)
                    act.activation(level(1), rest32[:, 2:4, :], ACT.Copy).then_inc(k_split, 1)

            def exps(phase, b, h, qp):
                it = h * 2 + qp
                start = filled_before(b) + it * phase.tiles
                mins = mins_before(b) + it * len(phase.mins)
                for tile in phase.act:
                    kind, u, n = tile
                    par, jj = u // UNITS, u % UNITS
                    if kind == "W":
                        act.wait_ge(low_ready, b * FH * NT + it * N_BODY + u + 1)
                        act.activation(fweight[:, u % 2, :], fmin[:, u % 2, :], ACT.Exp,
                                       bias=fnmax[:, u % 2:u % 2 + 1], scale=-1.0).then_inc(w_ready, 1)
                        continue
                    if kind == "Q":
                        act.wait_ge(filled, start + phase.fill_no[tile])
                        act.wait_ge(pv_done, (b * FH * NT + it * N_BODY + u) * 2)
                        act.activation(probsT[:, n // 2, (n % 2) * CH:(n % 2 + 1) * CH], bank(FP_BANK),
                                       ACT.Copy).then_inc(tile_read, 1)
                        continue
                    src = ring(phase.slot[tile])
                    if kind == "A":
                        act.wait_ge(min_ready, mins + phase.min_no[tile])
                        where = (slice(None), n % HALF, TPC * jj + n // HALF, ds(it * 2 + par, 1))
                        act.activation(src, src, ACT.Exp, bias=nmax[where], scale=-1.0,
                                       accum_out=esum[where]).then_inc(tile_read, 1)
                    elif kind == "F":
                        act.wait_ge(min_ready, mins + phase.min_no[tile])
                        act.activation(probs[:, n * TILE:(n + 1) * TILE], src, ACT.Exp,
                                       bias=fmin[:, u % 2, n:n + 1], scale=-1.0).then_inc(tile_read, 1)
                    else:
                        act.wait_ge(filled, start + phase.fill_no[tile])
                        act.wait_ge(pv_done, (b * FH * NT + it * N_BODY + u) * 2)
                        act.activation(probsT[:, n, :], src, ACT.Copy).then_inc(tile_read, 1)

            keys(0, ())
            with act.Fori(0, FH) as h:
                with act.Fori(0, 2) as qp:
                    exps(PA, None, h, qp)

            def join_halves(b):
                act.wait_ge(comb, b * COMB_STEPS + 2)
                act.activation(stats32[:, 1:3, :], stats32[:, 1:3, :], ACT.Exp).then_inc(comb_e, 1)

            join_halves(0)

            def copy_x(b, c):
                act.wait_ge(x_tr, (b * 2 + 1) * NCH + c + 1)
                if c < 2:
                    act.wait_ge(yp_ready, b * 2 * NCH)
                else:
                    act.wait_ge(v_ready, b * NCH + c - 1)
                chunk_copy(xT_ready, xT[c % 2], 0)

            copy_x(0, 0)
            copy_x(0, 1)

            def step(b, phase):
                def roots(n):
                    act.wait_ge(ln, n * LN_STEPS + 1)
                    act.activation(rstd[:, :], var[:, :], ACT.Sqrt).then_inc(ln_sq, 1)

                for c in range(NCH):
                    if c + 2 < NCH:
                        copy_x(b, c + 2)
                    act.wait_ge(o1_tr, b * 2 * NCH + c + 1)
                    act.wait_ge(yp_ready, b * 2 * NCH + c)
                    chunk_copy(o1T_ready, oT, 4)
                roots(b * 2)
                for c in range(NCH):
                    act.wait_ge(x1_tr, b * NCH + c + 1)
                    for cc in range(KC):
                        last = act.activation(x1T[:, cc, c * CH:(c + 1) * CH], bank(2 * (c % 2) + cc), ACT.Copy,
                                              accum_out=xsums[:, cc, c:c + 1])
                    last.then_inc(x1T_ready, 1)
                def router():
                    act.wait_ge(rt, b * ROUTE_STEPS + 3)
                    act.activation(route[:, NR:2 * NR], route[:, 0:NR], ACT.Exp, bias=route[:, 48:49],
                                   accum_out=route[:, 49:50]).then_inc(rt_e, 1)

                if phase is PAF:
                    keys(b + 1, ((n_out, (b * 2 + 1) * NCH * 16), (filled, filled_before(b))), router)
                else:
                    router()
                with act.Fori(0, NCH) as c:
                    k = b * PROJ + c
                    act.wait_ge(fp_read, k * 2 + 1)
                    act.activation(q_to(0, c), q32, ACT.Copy).then_inc(split_act, 1)
                    act.activation(q_to(2, c)[0:H], q32[0:H], ACT.Copy)
                    act.wait_ge(fsp, k)
                    act.wait_ge(fp_ready, k * 2 + 2)
                    act.activation(k32, bank(FP_BANK), ACT.Identity, bias=bqk_sel[:, 1:2]).then_inc(fp_read, 1)
                    act.wait_ge(fp_read, k * 2 + 2)
                    act.activation(k_to(0, c), k32, ACT.Copy).then_inc(split_act, 1)
                    act.wait_ge(split_dve, (b * NCH + c) * SPLIT_DVE + 1)
                    act.activation(q_to(1, c), q_rest, ACT.Copy).then_inc(split_act, 1)
                    act.wait_ge(split_dve, (b * NCH + c) * SPLIT_DVE + 2)
                    act.activation(fmid, k_rest, ACT.Copy).then_inc(split_act, 1)
                with act.Fori(0, FH) as h:
                    act.wait_ge(n_out, (b * 2 + 1) * NCH * 16)
                    if phase is PAF:
                        act.wait_ge(q_split, (b + 2) * NCH * Q_STEPS)
                        act.wait_ge(k_split, (b + 2) * NCH * K_STEPS)
                    with act.Fori(0, 2) as qp:
                        exps(phase, b, h, qp)
                if phase is PAF:
                    join_halves(b + 1)
                act.wait_ge(fsp, (b + 1) * PROJ)
                for c in range(NCH):
                    k = (b * 2 + 1) * NCH + c
                    act.wait_ge(o1_tr, k + 1)
                    if c >= 2:
                        act.wait_ge(yp_ready, k - 1)
                    chunk_copy(o1T_ready, xT[c % 2], 2 * (c % 2))
                if phase is PAF:
                    copy_x(b + 1, 0)
                    copy_x(b + 1, 1)
                roots(b * 2 + 1)

            next_batches(act, step)

        @block.vector
        def _(dve):
            v_b_in = b_in_rows[:, :].rearrange("p (h c i) -> p c h i", h=AH, c=3)
            dve.wait_ge(const_in, 16 * N_CONST)
            for c in range(2):
                last = dve.tensor_copy(buf_c[0:1, c * D:(c + 1) * D].rearrange("p (h i) -> p h i", h=AH),
                                       v_b_in[0:1, c, :, :])
            last.then_inc(wT_read, 1)
            dve.wait_ge(wT_ready, 1)
            for cc in range(KC):
                nat = ps[:, 2 * cc:2 * cc + 2, :].rearrange("p a n -> p (a n)")[:, 0:3 * D].rearrange(
                    "p (h c i) -> p c h i", h=AH, c=3)
                for c in range(3):
                    dve.tensor_copy(w_inT[:, cc, c * D:(c + 1) * D].rearrange("p (h i) -> p h i", h=AH),
                                    nat[:, c, :, :])
                last = dve.tensor_copy(w_outT[:, cc, :], ps[:, 4 + cc, 0:D])
            last.then_inc(wT_read, 1)
            dve.wait_ge(wT_ready, 2)
            dve.tensor_copy(qk_bias[:, :], ps[:, 6, 0:4]).then_inc(wT_read, 1)
            dve.wait_ge(wT_read, 3)

            def queries(b, free, used):
                with dve.Fori(0, NCH) as c:
                    k = b * NCH + c
                    level = lambda lv: split[:, 0, :, lv, ds(c * CH, CH)]
                    queries, rest = qk32[:, 0:2, :], rest32[:, 0:2, :]
                    for what, count in free:
                        dve.wait_ge(what, count)
                    dve.wait_ge(filled, used)
                    dve.wait_ge(qk_ready, k * 4 + 2)
                    dve.wait_ge(q_split, k * Q_STEPS)
                    for s in range(2):
                        last = dve.tensor_scalar(qk32[:, s, :], bank(2 + s), qk_bias[:, s:s + 1],
                                                 -float(AD) ** -0.5, ALU.add, ALU.mult)
                    last.then_inc(q32_ready, 1)
                    dve.wait_ge(q32_ready, k + 1)
                    dve.tensor_copy(level(0), queries).then_inc(q_split, 1)
                    dve.wait_ge(q_split, k * Q_STEPS + 1)
                    dve.tensor_tensor(rest, queries, level(0), ALU.subtract).then_inc(q_split, 1)
                    dve.wait_ge(q_split, k * Q_STEPS + 2)
                    dve.tensor_copy(level(1), rest).then_inc(q_split, 1)
                    dve.wait_ge(q_split, k * Q_STEPS + 3)
                    dve.tensor_tensor(level(2), rest, level(1), ALU.subtract).then_inc(q_split, 1)

            def read_chunk(b, hh, c, s):
                k = b * PROJ + hh * NCH + c
                if s == 0:
                    dve.wait_ge(fsp, k)
                dve.wait_ge(fp_ready, k * 2 + s + 1)
                dve.tensor_scalar(f32s[:, s, :], bank(FP_BANK), bqk_sel[:, s:s + 1],
                                  -float(FD) ** -0.5 if s == 0 else 1.0, ALU.add, ALU.mult).then_inc(fp_read, 1)

            def minima(phase, b, h, qp):
                it = h * 2 + qp
                start = filled_before(b) + it * phase.tiles
                units = 0 if b is None else b * FH * NT + it * N_BODY
                for tile in phase.dve:
                    kind, u, n = tile
                    par, jj = u // UNITS, u % UNITS
                    if kind in "AF":
                        dve.wait_ge(filled, start + phase.fill_no[tile])
                        src = ring(phase.slot[tile])
                    if kind == "A":
                        dve.tensor_reduce(nmax[:, n % HALF, TPC * jj + n // HALF, ds(it * 2 + par, 1)],
                                          src, AX.X, ALU.min).then_inc(min_ready, 1)
                    elif kind == "F":
                        dve.tensor_reduce(fmin[:, u % 2, n:n + 1], src, AX.X, ALU.min).then_inc(min_ready, 1)
                        if n == 1:
                            dve.drain()
                            dve.tensor_reduce(fnmax[:, u % 2:u % 2 + 1], fmin[:, u % 2, :], AX.X,
                                              ALU.min).then_inc(low_ready, 1)
                    elif kind == "P":
                        read_chunk(b, h + 1, qp * 2 + par, n)
                    else:
                        dve.wait_ge(w_ready, units + u + 1)
                        dve.wait_ge(pv_done, (units + u + 1) * 2)
                        for half in range(HALF):
                            part = ps[:, O_BANK, half * (FD + 1):(half + 1) * (FD + 1)]
                            weight = fweight[:, u % 2, half:half + 1]
                            if half == 0:
                                dve.tensor_scalar(fsum[:, :], part, weight, None, ALU.mult)
                            else:
                                dve.scalar_tensor_tensor(fsum[:, :], part, weight, fsum[:, :], ALU.mult, ALU.add)
                            dve.drain()
                        dve.reciprocal(frec[:, :], fsum[:, FD:FD + 1])
                        dve.drain()
                        dve.tensor_scalar(fo[:, ds(qp * N_BODY + u, 1), ds(h * FD, FD)],
                                          fsum[:, 0:FD], frec[:, :], None, ALU.mult).then_inc(o_read, 1)

            queries(0, (), 0)
            with dve.Fori(0, FH) as h:
                with dve.Fori(0, 2) as qp:
                    minima(PA, None, h, qp)

            def join_halves(b):
                n = NT * AH
                lows = nmax[:, :, :, :].rearrange("p f t a -> p f (t a)")
                sums = esum[:, :, :, :].rearrange("p f t a -> p f (t a)")
                base = b * COMB_STEPS
                dve.wait_ge(tile_read, filled_before(b) + CREDIT)
                dve.tensor_tensor(stats32[:, 0, :], lows[:, 0, :], lows[:, 1, :], ALU.min).then_inc(comb, 1)
                dve.wait_ge(comb, base + 1)
                dve.tensor_tensor(stats32[:, 1:3, :], stats32[:, 0:1, :].to_broadcast([P, HALF, n]), lows,
                                  ALU.subtract).then_inc(comb, 1)
                dve.wait_ge(comb_e, b + 1)
                dve.tensor_tensor(stats32[:, 1:3, :], stats32[:, 1:3, :], sums, ALU.mult).then_inc(comb, 1)
                dve.wait_ge(comb, base + 3)
                dve.tensor_tensor(stats32[:, 3, :], stats32[:, 1, :], stats32[:, 2, :], ALU.add).then_inc(comb, 1)
                dve.wait_ge(comb, base + 4)
                dve.reciprocal(stats32[:, 4, :], stats32[:, 3, :]).then_inc(comb, 1)
                dve.wait_ge(comb, base + 5)
                dve.tensor_tensor(att[:, :, :].rearrange("p t a -> p (t a)"), stats32[:, 3, :], stats32[:, 4, :],
                                  ALU.mult).then_inc(comb, 1)
                dve.drain()

            join_halves(0)

            def step(b, phase):
                def add_rows(k, c, rows, bank0):
                    dve.wait_ge(yp_ready, k + 1)
                    dve.wait_ge(res_ready, k + 1)
                    for j in range(2):
                        last = dve.tensor_tensor(y[:, ds(c * TPC + 2 * j, 2), :], bank_rows(bank0 + j),
                                                 rows[:, ds(c * TPC + 2 * j, 2), :], ALU.add)
                    last.then_inc(y_ready, 1)
                    dve.drain()
                    for t in range(TPC):
                        last = dve.bn_stats(st[:, t, :], flat(y[:, ds(c * TPC + t, 1), :]))
                    last.then_inc(bn_ready, 1)
                    dve.drain()
                    for t in range(TPC):
                        last = dve.bn_aggr(mv_chunk[:, t, :], st[:, t, :])
                    last.then_inc(bn_ready, 1)
                    dve.wait_ge(bn_ready, k * BN_STEPS + 2)
                    dve.tensor_copy(mv[:, ds(c * TPC, TPC), :], mv_chunk[:, :, :]).then_inc(bn_ready, 1)
                    dve.wait_ge(bn_ready, k * BN_STEPS + 3)

                def norm_factors(n):
                    base = n * LN_STEPS
                    dve.tensor_scalar(var[:, :], mv[:, :, 1], EPS, None, ALU.add).then_inc(ln, 1)
                    dve.wait_ge(ln_sq, n + 1)
                    dve.reciprocal(rstd[:, :], rstd[:, :]).then_inc(ln, 1)
                    dve.wait_ge(ln, base + 2)
                    dve.tensor_tensor(newt[:, :], rstd[:, :], rstd[:, :], ALU.mult).then_inc(ln, 1)
                    dve.wait_ge(ln, base + 3)
                    dve.tensor_tensor(newt[:, :], newt[:, :], var[:, :], ALU.mult).then_inc(ln, 1)
                    dve.wait_ge(ln, base + 4)
                    dve.tensor_scalar(newt[:, :], newt[:, :], -0.5, 1.5, ALU.mult, ALU.add).then_inc(ln, 1)
                    dve.wait_ge(ln, base + 5)
                    dve.tensor_tensor(rstd[:, :], rstd[:, :], newt[:, :], ALU.mult).then_inc(ln, 1)
                    dve.drain()

                def norm_chunk(c):
                    for t in range(TPC):
                        at = c * TPC + t
                        rows = flat(y[:, ds(at, 1), :])
                        last = dve.tensor_scalar(rows, rows, mv[:, ds(at, 1), 0],
                                                 rstd[:, ds(at, 1)], ALU.subtract, ALU.mult)
                    last.then_inc(n_ready, TPC)

                def attend(c):
                    heads = lambda ap: ap.rearrange("p t (h i) -> p t h i", h=AH)
                    out_rows = heads(fo[:, ds(c * TPC, TPC), :])
                    dve.wait_ge(v_ready, b * NCH + c + 1)
                    dve.wait_ge(o1_tr, b * 2 * NCH)
                    for j in range(2):
                        last = dve.tensor_tensor(out_rows[:, 2 * j:2 * j + 2], heads(bank_rows(2 + j)),
                                                 v_b_in[:, 2:3, :, :].to_broadcast([P, 2, AH, AD]), ALU.add)
                    last.then_inc(v_read, 1)
                    dve.wait_ge(v_read, b * NCH + c + 1)
                    dve.tensor_tensor(out_rows, out_rows,
                                      att[:, ds(c * TPC, TPC), :].unsqueeze(3).to_broadcast([P, TPC, AH, AD]),
                                      ALU.mult).then_inc(o1_ready, 1)

                attend(0)
                with dve.Fori(0, NCH - 1) as c:
                    attend(c + 1)
                    dve.wait_ge(n_out, b * 2 * NCH * 16)
                    dve.wait_ge(k_split, (b + 1) * NCH * K_STEPS)
                    add_rows(b * 2 * NCH + c, c, rows_q, 6)
                add_rows(b * 2 * NCH + NCH - 1, NCH - 1, rows_q, 6)
                norm_factors(b * 2)
                with dve.Fori(0, NCH) as c:
                    norm_chunk(c)

                base = b * ROUTE_STEPS
                logits, probs_r = route[:, 0:NR], route[:, NR:2 * NR]
                best, order, low, total, rec, back = (route[:, 32:40], route[:, 40:48], route[:, 48:49],
                                                      route[:, 49:50], route[:, 50:51], route[:, 52:60])
                dve.wait_ge(x1T_ready, (b + 1) * NCH)
                dve.tensor_reduce(xsum[:, :], xsums[:, :, :], AX.X, ALU.add).then_inc(rt, 1)
                dve.wait_ge(rt_mm, b + 1)
                dve.scalar_tensor_tensor(logits, ps[0:1, 6, 0:NR], 1.0 / L, br_row[:, :],
                                         ALU.mult, ALU.add).then_inc(rt, 1)
                dve.wait_ge(rt, base + 2)
                dve.tensor_reduce(low, logits, AX.X, ALU.max, negate=True).then_inc(rt, 1)
                dve.wait_ge(rt_e, b + 1)
                dve.reciprocal(rec, total).then_inc(rt, 1)
                dve.wait_ge(rt, base + 4)
                dve.tensor_scalar(probs_r, probs_r, rec, None, ALU.mult).then_inc(rt, 1)
                dve.drain()
                dve.max(best, probs_r).then_inc(rt, 1)
                dve.drain()
                dve.max_index(top_i[:, :], best, probs_r).then_inc(rt, 1)
                dve.wait_ge(rt, base + 7)
                dve.tensor_copy(order, top_i[:, :]).then_inc(rt, 1)
                dve.wait_ge(rt, base + 8)
                dve.memset(order[:, FH:8], -float(NR))
                dve.tensor_scalar(order[:, 0:FH], order[:, 0:FH], -1.0, None, ALU.mult).then_inc(rt, 1)
                dve.drain()
                dve.max(back, order).then_inc(rt, 1)
                dve.wait_ge(rt, base + 10)
                dve.tensor_scalar(head_i[:, :], back, -1.0, None, ALU.mult).then_inc(rt, 1)

                if phase is PAF:
                    queries(b + 1, ((n_out, (b * 2 + 1) * NCH * 16),), filled_before(b))
                with dve.Fori(0, NCH // 2) as pair:
                    for half in range(2):
                        c = pair * 2 + half
                        steps = (b * NCH + c) * SPLIT_ACT
                        if phase is PAF:
                            dve.wait_ge(x_tr, (b * 2 + 3) * NCH)
                            dve.wait_ge(qk_ready, (b + 2) * NCH * 4)
                        dve.wait_ge(o1T_ready, (b * 2 + 1) * NCH)
                        read_chunk(b, 0, c, 0)
                        dve.wait_ge(split_act, steps + 1)
                        dve.tensor_tensor(q_rest, q32, q_to(0, c), ALU.subtract).then_inc(split_dve, 1)
                        dve.wait_ge(wv_in, (b + 1) * 2 * FH * 16)
                        dve.wait_ge(fv_ready, b * NCH + c + 1)
                        for t in range(TPC):
                            last = dve.tensor_tensor(
                                vals[:, ds(c * TPC + t, 1), :, 0:FD].rearrange("p a h n -> p (a h) n"),
                                ps[:, 2 + 2 * half + t // 2, (t % 2) * D:(t % 2 + 1) * D].rearrange("p (h n) -> p h n", h=FH),
                                bv_sel[:, :].rearrange("p (h n) -> p h n", h=FH), ALU.add)
                        last.then_inc(fv_read, 1)
                        dve.wait_ge(split_act, steps + 2)
                        dve.tensor_tensor(k_rest, k32, k_to(0, c), ALU.subtract).then_inc(split_dve, 1)
                        dve.tensor_copy(k_to(1, c)[H:P], k32[H:P])
                        dve.wait_ge(split_act, steps + 3)
                        dve.tensor_tensor(q_to(2, c)[H:P], q_rest[H:P], q_to(1, c)[H:P], ALU.subtract)
                        dve.wait_ge(split_act, steps + 4)
                        dve.tensor_tensor(k_to(1, c)[0:H], k_rest[0:H], fmid[0:H, :], ALU.subtract)
                        dve.tensor_copy(k_to(0, c)[H:P], fmid[H:P, :]).then_inc(fsp, 1)
                with dve.Fori(0, FH) as h:
                    with dve.Fori(0, 2) as qp:
                        minima(phase, b, h, qp)

                if phase is PAF:
                    join_halves(b + 1)
                with dve.Fori(0, NCH // 2) as pair:
                    for half in range(2):
                        c = pair * 2 + half
                        add_rows((b * 2 + 1) * NCH + c, c, rows_k, 4 + 2 * half)
                norm_factors(b * 2 + 1)
                with dve.Fori(0, NCH) as c:
                    norm_chunk(c)

            next_batches(dve, step)


_INS = ["x", "w_in", "b_in", "w_out", "b_out"]
_ALL = ["L0_attn_" + n for n in _INS] + ["L0_ffn_" + n for n in
                                         ("Wq", "bq", "Wk", "bk", "Wv", "bv", "Wr", "br", "Wo", "bo")]


def kernel(**inputs):
    import numpy as _np
    import concourse.bacc as _bacc
    from concourse import mybir as _mybir
    from concourse.bass_utils import run_bass_kernel_spmd as _run

    nc = _bacc.Bacc("TRN2", target_bir_lowering=False, num_devices=1)
    arrays, args = {}, []
    for name in _ALL:
        a = _np.ascontiguousarray(inputs[name])
        arrays[f"in_{name}"] = a
        args.append(nc.dram_tensor(f"in_{name}", a.shape, _mybir.dt.from_np(a.dtype), kind="ExternalInput").ap())
    out = nc.dram_tensor("out_rows", (B, L, D), _mybir.dt.float32, kind="ExternalOutput").ap()
    build(nc, *args, out)
    r = _run(nc, [arrays], core_ids=[0])
    return r.results[0]["out_rows"]
```
